# Optimizing a Trainium2 kernel written in Bass

```python
import numpy as np
import jax
import jax.numpy as jnp

def _softmax(x, axis=-1):
    return jax.nn.softmax(x, axis=axis)

def _gelu(x):
    return jax.nn.gelu(x, approximate=True)

def _silu(x):
    return jax.nn.silu(x)

def _sigmoid(x):
    return jax.nn.sigmoid(x)

def _layernorm(x, axis=-1, eps=1e-05):
    m = jnp.mean(x, axis=axis, keepdims=True)
    v = jnp.var(x, axis=axis, keepdims=True)
    return (x - m) / jnp.sqrt(v + eps)

def _scatter_add(tgt, idx, src, axis=0):
    return tgt.at[idx].add(src)

def _segment_sum(src, seg, n):
    return jax.ops.segment_sum(src, seg, n)
kernel_name = 'mk_metaformer_d1_conv_nchw256_r4_142b62'

def setup_inputs(seed: int=0):
    np.random.seed(seed)
    _w = jnp.asarray

    def _rec_inputs():
        import jax
        import jax.numpy as jnp
        _gk = jax.random.key(seed)
        x = -0.0003929 + 0.9999 * jax.random.normal(jax.random.fold_in(_gk, 1), (16, 64, 32, 32), jnp.float32)
        return x
    x = _rec_inputs()

    def _L0_conv_setup():
        import jax, jax.numpy as jnp
        import numpy as np
        from jax import lax
        DN = ('NCHW', 'OHWI', 'NCHW')
        key = jax.random.key(seed)
        k1, k2 = jax.random.split(key)
        N, C_IN, H, W, C_OUT, K = (16, 64, 32, 32, 64, 3)
        x = jax.random.normal(k1, (N, C_IN, H, W), dtype=jnp.float32)
        stdv = 1.0 / np.sqrt(C_IN * K * K)
        weight = jax.random.uniform(k2, (C_OUT, K, K, C_IN), dtype=jnp.float32, minval=-stdv, maxval=stdv)
        return {'x': x, 'weight': weight}
    _L0_conv_all = _L0_conv_setup()
    _L0_conv_in = {k: v for k, v in _L0_conv_all.items() if k in ('weight',)}
    del _L0_conv_all

    def _L0_ffn_setup():
        import math
        import jax, jax.numpy as jnp
        import numpy as np
        CAPACITY_FACTOR = 1.25
        TOP_K = 2
        LN_EPS = 1e-05

        def _layer_norm(x, gamma, beta):
            mu = jnp.mean(x, axis=-1, keepdims=True)
            var = jnp.var(x, axis=-1, keepdims=True)
            return (x - mu) * jax.lax.rsqrt(var + LN_EPS) * gamma + beta
        key = jax.random.key(seed)
        ks = jax.random.split(key, 4)
        B, S, D, F, E = (8, 1024, 64, 128, 8)
        x = jax.random.normal(ks[0], (B, S, D), dtype=jnp.float32)
        Wr = jax.random.normal(ks[1], (D, E), dtype=jnp.float32) / np.sqrt(D)
        br = jnp.zeros((E,), jnp.float32)
        W1 = jax.random.normal(ks[2], (E, D, F), dtype=jnp.float32) / np.sqrt(D)
        b1 = jnp.zeros((E, F), jnp.float32)
        W2 = jax.random.normal(ks[3], (E, F, D), dtype=jnp.float32) / np.sqrt(F)
        b2 = jnp.zeros((E, D), jnp.float32)
        gamma = jnp.ones((D,), jnp.float32)
        beta = jnp.zeros((D,), jnp.float32)
        return {'x': x, 'Wr': Wr, 'br': br, 'W1': W1, 'b1': b1, 'W2': W2, 'b2': b2, 'gamma': gamma, 'beta': beta}
    _L0_ffn_all = _L0_ffn_setup()
    _L0_ffn_in = {k: v for k, v in _L0_ffn_all.items() if k in ('Wr', 'br', 'W1', 'b1', 'W2', 'b2', 'gamma', 'beta')}
    del _L0_ffn_all
    return {'x': x, 'L0_conv_weight': _L0_conv_in['weight'], 'L0_ffn_Wr': _L0_ffn_in['Wr'], 'L0_ffn_br': _L0_ffn_in['br'], 'L0_ffn_W1': _L0_ffn_in['W1'], 'L0_ffn_b1': _L0_ffn_in['b1'], 'L0_ffn_W2': _L0_ffn_in['W2'], 'L0_ffn_b2': _L0_ffn_in['b2'], 'L0_ffn_gamma': _L0_ffn_in['gamma'], 'L0_ffn_beta': _L0_ffn_in['beta']}

def reference(x, L0_conv_weight, L0_ffn_Wr, L0_ffn_br, L0_ffn_W1, L0_ffn_b1, L0_ffn_W2, L0_ffn_b2, L0_ffn_gamma, L0_ffn_beta):
    import jax
    import jax.numpy as jnp

    def _L0_conv_ref(x, weight):
        import jax, jax.numpy as jnp
        import numpy as np
        from jax import lax
        DN = ('NCHW', 'OHWI', 'NCHW')
        xb = jnp.sign(x)
        wb = jnp.sign(weight)
        conv_sum = lax.conv_general_dilated(xb, wb, window_strides=(1, 1), padding=[(1, 1), (1, 1)], dimension_numbers=DN)
        xpad = jnp.pad(xb, ((0, 0), (0, 0), (0, 0), (1, 1)))
        xprod = xpad[..., :-2] * xpad[..., 1:-1] * xpad[..., 2:]
        wprod = jnp.prod(wb, axis=2)[:, :, None, :]
        conv_prod = lax.conv_general_dilated(xprod, wprod, window_strides=(1, 1), padding=[(1, 1), (0, 0)], dimension_numbers=DN)
        return 0.5 * (conv_sum - conv_prod)

    def _L0_ffn_ref(x, Wr, br, W1, b1, W2, b2, gamma, beta):
        import math
        import jax, jax.numpy as jnp
        import numpy as np
        CAPACITY_FACTOR = 1.25
        TOP_K = 2
        LN_EPS = 1e-05

        def _layer_norm(x, gamma, beta):
            mu = jnp.mean(x, axis=-1, keepdims=True)
            var = jnp.var(x, axis=-1, keepdims=True)
            return (x - mu) * jax.lax.rsqrt(var + LN_EPS) * gamma + beta
        B, S, D = x.shape
        E = Wr.shape[1]
        N = B * S
        K = TOP_K
        logits = jnp.mean(x, axis=1) @ Wr + br
        routing_weights = jax.nn.softmax(logits, axis=-1)
        capacity = float(math.ceil(N * CAPACITY_FACTOR / E))
        expected_loads = routing_weights.sum(axis=0) * (N / B)
        scale = jnp.where(expected_loads > capacity, capacity / expected_loads, 1.0)
        routing_weights = jax.nn.softmax(routing_weights * scale, axis=-1)
        rw_tok = jnp.broadcast_to(routing_weights[:, None, :], (B, S, E)).reshape(N, E)
        top_w, top_i = jax.lax.top_k(rw_tok, K)
        top_w = jax.nn.softmax(top_w, axis=-1)
        xf = x.reshape(N, D)
        h = jax.nn.gelu(jnp.einsum('nd,edf->enf', xf, W1) + b1[:, None, :], approximate=False)
        y = jnp.einsum('enf,efd->end', h, W2) + b2[:, None, :]
        w_dense = jnp.zeros((N, E), x.dtype).at[jnp.arange(N)[:, None], top_i].add(top_w)
        out = jnp.einsum('ne,end->nd', w_dense, y).reshape(B, S, D)
        out = _layer_norm(out + x, gamma, beta)
        return out

    def _gn(v, G=32, eps=1e-05):
        B_, C_, H_, W_ = v.shape
        g = v.reshape(B_, G, C_ // G, H_, W_)
        m = jnp.mean(g, axis=(2, 3, 4), keepdims=True)
        s = jnp.var(g, axis=(2, 3, 4), keepdims=True)
        return ((g - m) / jnp.sqrt(s + eps)).reshape(v.shape)

    def _ln_c(v, eps=1e-06):
        m = jnp.mean(v, axis=1, keepdims=True)
        s = jnp.var(v, axis=1, keepdims=True)
        return (v - m) / jnp.sqrt(s + eps)

    def _ln_t(v, eps=1e-05):
        m = jnp.mean(v, axis=-1, keepdims=True)
        s = jnp.var(v, axis=-1, keepdims=True)
        return (v - m) / jnp.sqrt(s + eps)

    def _to_tokens(v):
        B_, C_, H_, W_ = v.shape
        return v.reshape(B_, C_, H_ * W_).transpose(0, 2, 1)

    def _from_tokens(t, like):
        B_, C_, H_, W_ = like.shape
        return t.transpose(0, 2, 1).reshape(B_, C_, H_, W_)
    x = x + _L0_conv_ref(_ln_c(x), L0_conv_weight)
    t = _to_tokens(x)
    t = t + _L0_ffn_ref(_ln_t(t), L0_ffn_Wr, L0_ffn_br, L0_ffn_W1, L0_ffn_b1, L0_ffn_W2, L0_ffn_b2, L0_ffn_gamma, L0_ffn_beta)
    x = _from_tokens(t, x)
    return x

_drawn_inputs = setup_inputs


def setup_inputs(seed=0):
    import zlib

    import numpy as np

    out = dict(_drawn_inputs(seed))
    spreads = {'L0_ffn_br': (0.0, 0.1),
     'L0_ffn_b1': (0.0, 0.8),
     'L0_ffn_b2': (0.0, 0.8),
     'L0_ffn_gamma': (1.0, 0.6),
     'L0_ffn_beta': (0.0, 0.8)}
    factors = {'L0_ffn_Wr': 8.0}
    for name, (base, spread) in spreads.items():
        noise = np.random.default_rng([zlib.crc32(name.encode()), seed]).standard_normal(out[name].shape)
        drawn = base * np.exp(spread * noise) if base else spread * noise
        out[name] = jnp.asarray(drawn.astype(out[name].dtype))
    for name, factor in factors.items():
        out[name] = (out[name] * factor).astype(out[name].dtype)
    return out
```

```python
from contextlib import ExitStack

import numpy as np

import concourse.bass as bass
from concourse import mybir

N_IMG, CH, H, W = 16, 64, 32, 32
TOK = H * W
PAIRS = N_IMG // 2
EXPERTS, FFN = 8, 128
HALF = TOK // 2
ROWS_HALF = H // 2
PW = W + 2
PADDED = (H + 2) * PW
REGIONS = 2 * PADDED
QUARTER = TOK // 4
EPS_LN = 1e-5
CAPACITY = float(-(-N_IMG * TOK * 5 // (4 * EXPERTS)))
RSTD_SCALE = 128.0
W1_SCALE = 64.0

C_CENTER, C_SUM, C_IOTA8, C_PART, C_EYE, C_ONES = 0, 128, 160, 168, 169, 185
C32 = C_ONES + 128
C_NEGMEAN, C_SPREAD, C_ID16 = 0, 128, 640
C16 = C_ID16 + 64


ROUTE_GAP, ROUTE_DIAG, ROUTE_OFFS, ROUTE_HOT, ROUTE_DENSE, ROUTE_B1, ROUTE_LAST = 19, 26, 29, 30, 32, 33, 34
ZERO_OF = [0, 1, 1, 1, 3, 3, 3, 3]


def constants():
    c = np.zeros((128, C32), np.float32)
    for b in (0, 64):
        c[b:b + 64, C_CENTER + b:C_CENTER + b + 64] = np.eye(64) - 1.0 / CH
        c[b:b + 64, C_SUM + b // 64] = 1.0 / CH
    c[:, C_IOTA8:C_IOTA8 + 8] = np.arange(8) - 8
    c[:, C_PART] = np.arange(128)
    c[0:16, C_EYE:C_EYE + 16] = np.eye(16)
    c[:, C_ONES:C_ONES + 128] = 1.0
    d = np.zeros((128, C16), np.float16)
    for b in (0, 64):
        d[b:b + 64, C_NEGMEAN + b:C_NEGMEAN + b + 64] = -1.0 / CH
    for j in range(4):
        for b in (0, 1):
            for part in (0, 2):
                d[32 * j + part + b, C_SPREAD + 128 * j + 64 * b:C_SPREAD + 128 * j + 64 * b + 64] = 1 / RSTD_SCALE
    d[0:64, C_ID16:C_ID16 + 64] = np.eye(64)
    return c, d


def metaformer(nc, x, conv_w, Wr, br, W1, b1, W2, b2, gamma, beta, const32, const16, out):
    F32, F16, I32, F8 = mybir.dt.float32, mybir.dt.float16, mybir.dt.int32, mybir.dt.float8e4
    ALU, ACT, AX = mybir.AluOpType, mybir.ActivationFunctionType, mybir.AxisListType
    LO, HI = slice(0, 64), slice(64, 128)
    IMG = (LO, HI)

    x_pairs = x.rearrange("(q b) c h w -> q (b c) (h w)", b=2)
    out_pairs = out.rearrange("(q b) c h w -> q (b c) (h w)", b=2)

    with ExitStack() as ctx:
        def sb(name, shape, dt=F32):
            return ctx.enter_context(nc.sbuf_tensor(name, shape, dt))

        def sem(name):
            return ctx.enter_context(nc.semaphore(name))

        xs = sb("xs", [128, PAIRS, TOK])
        us = sb("us", [128, PAIRS, TOK])
        conv16 = sb("conv16", [128, PAIRS, TOK], F16)
        split = sb("split", [128, PAIRS, 2, TOK], F16)
        signs = sb("signs", [128, PAIRS, REGIONS], F8)
        stack = sb("stack", [128, 3, 2, REGIONS], F8)
        edge = sb("edge", [128, PADDED], F16)
        uh = sb("uh", [128, TOK], F16)
        ul = sb("ul", [128, TOK], F16)
        sq = sb("sq", [128, TOK])
        hid = sb("hid", [128, 2, 2, TOK])
        var_t = sb("var_t", [128, QUARTER])
        var_c = sb("var_c", [128, 8, 2])
        rstd_c = sb("rstd_c", [128, 8, 2])
        neg_half = sb("neg_half", [128, 16])
        rstd_s = sb("rstd_s", [128, 8, 32], F16)
        rstd_t = sb("rstd_t", [128, QUARTER], F16)
        c32 = sb("c32", [128, C32])
        c16 = sb("c16", [128, C16], F16)
        cw = sb("cw", [64, 3, 3, 64])
        cws = sb("cws", [64, 3, 3, 64], F16)
        cwp = sb("cwp", [64, 3, 64], F16)
        cwo = sb("cwo", [64, 2, 3, 2, 2, 64], F16)
        cwT = sb("cwT", [128, 2, 3, 2, 64], F16)
        w1f = sb("w1f", [128, EXPERTS, FFN])
        w1s = sb("w1s", [128, EXPERTS, 2, FFN], F16)
        w2f = sb("w2f", [128, EXPERTS, CH])
        w2m = sb("w2m", [128, EXPERTS])
        w2sel = sb("w2sel", [128, 2, 2, PAIRS, CH])
        b1f = sb("b1f", [EXPERTS, FFN])
        b2f = sb("b2f", [EXPERTS, CH])
        b2m = sb("b2m", [EXPERTS, 1])
        wr = sb("wr", [128, EXPERTS])
        brs = sb("brs", [N_IMG, EXPERTS])
        gam = sb("gam", [128, 1])
        bet = sb("bet", [128, 1])
        usum = sb("usum", [128, PAIRS])
        ublk = sb("ublk", [128, 2, PAIRS])
        rt = sb("rt", [N_IMG, 16, 8])
        rc = sb("rc", [N_IMG, 16])
        diag = sb("diag", [N_IMG, 2, 2, N_IMG])
        picks = sb("picks", [128, 2, 2, N_IMG])
        offs = sb("offs", [1, 2, 32], I32)
        hot = sb("hot", [EXPERTS, 32])
        wden = sb("wden", [EXPERTS, 2, N_IMG])
        b1sel = sb("b1sel", [128, 32])
        b2sel = sb("b2sel", [128, PAIRS])

        ps = ctx.enter_context(nc.psum_tensor("ps", [128, 8, 512], F32))
        cen_ps = ps[:, 0:2, :]
        conv_ps = ps[:, 2:4, :]
        var_ps = ps[:, 4, 0:QUARTER]
        spread_ps = ps[:, 5:7, :]
        misc_ps = ps[:, 7, :]
        hid_ps = (ps[:, 0:2, :], ps[:, 2:4, :])
        y_ps = ps[:, 5:7, :]
        spread2_ps = ps[:, 7, :]

        s_x = [sem(f"x_loaded{p}") for p in range(PAIRS)]
        s_const = sem("const_loaded")
        s_cw = sem("conv_weights_loaded")
        s_w1 = sem("w1_loaded")
        s_w = sem("weights_loaded")
        s_zero = sem("zeroed")
        s_zero_v = sem("rstd_columns_zeroed")
        s_cw_sign = sem("conv_weight_signs")
        s_cw_prep = sem("conv_weight_steps")
        s_cw_ord = sem("conv_weights_ordered")
        s_cw_tr = sem("conv_weights_turned")
        s_cw_done = sem("conv_weights_ready")
        s_w1h = sem("w1_high")
        s_w1l = sem("w1_low")
        s_w2c = sem("w2_steps")
        s_cen = sem("centred")
        s_sign = sem("signs_done")
        s_keep = sem("centred_kept")
        s_edge = sem("edge_products")
        s_prod = sem("products_done")
        s_stack = [sem(f"stacked{b}") for b in range(3)]
        s_conv = sem("conv_done")
        s_c16 = sem("conv16_done")
        s_cc = sem("conv_centred")
        s_xc = sem("residual_centred")
        s_sq = sem("squares_done")
        s_var = sem("variances_done")
        s_vt = sem("variances_turned")
        s_vc = sem("variances_compact")
        s_pow = sem("rstd_done")
        s_rh = sem("rstd_high")
        s_rl = sem("rstd_low")
        s_rt = sem("rstd_rows")
        s_sp = sem("rstd_spread")
        s_u = sem("tokens_done")
        s_uh = sem("token_high")
        s_ul = sem("token_low")
        s_split = [sem(f"token_split{p}") for p in range(PAIRS)]
        s_ublk = sem("token_sums")
        s_route_pe = sem("route_products")
        s_route_dve = sem("route_vector_steps")
        s_route_act = sem("route_scalar_steps")
        s_res = sem("residual_done")
        s_w2s = sem("w2_selected")
        s_up = sem("up_projected")
        s_gelu = sem("hidden_done")
        s_down = sem("down_projected")
        s_z = sem("mixture_centred")
        s_zr = sem("normalised")
        s_sp2 = sem("rstd_spread2")
        s_o = sem("output_done")
        s_out = sem("output_stored")

        block = ctx.enter_context(nc.Block())

        SIGN_AT = lambda b, p: signs[IMG[b], p, :]

        def padded(ap):
            return ap.rearrange("q (r c) -> q r c", c=PW)

        @block.sync
        def _(sp):
            sp.dma_start(c32[:], const32).then_inc(s_const, 16)
            for p in range(2):
                sp.dma_start(xs[:, p, :], x_pairs[p]).then_inc(s_x[p], 16)
            sp.dma_start(cw[:], conv_w).then_inc(s_cw, 16)
            sp.dma_start(c16[:], const16).then_inc(s_const, 16)
            for p in range(2, 4):
                sp.dma_start(xs[:, p, :], x_pairs[p]).then_inc(s_x[p], 16)
            for b in range(2):
                sp.dma_start(w1f[IMG[b], :, :], W1.rearrange("e d f -> d e f")).then_inc(s_w1, 16)
            sp.dma_start(w2f[:], W2.rearrange("e f d -> f e d")).then_inc(s_w, 16)
            sp.dma_start(b1f[:], b1).then_inc(s_w, 16)
            sp.dma_start(b2f[:], b2).then_inc(s_w, 16)
            sp.dma_start(brs[:], br.rearrange("(o e) -> o e", o=1).broadcast_to([N_IMG, EXPERTS])).then_inc(s_w, 16)
            for b in range(2):
                sp.dma_start(wr[IMG[b], :], Wr).then_inc(s_w, 16)
                sp.dma_start(gam[IMG[b], :], gamma.rearrange("(d o) -> d o", o=1)).then_inc(s_w, 16)
                sp.dma_start(bet[IMG[b], :], beta.rearrange("(d o) -> d o", o=1)).then_inc(s_w, 16)

            def stack_pair(p):
                sp.wait_ge(s_prod, p + 1)
                if p >= 3:
                    sp.wait_ge(s_conv, 2 * (p - 2))
                for b in range(2):
                    src = signs[IMG[b], p, :]
                    sp.dma_start(stack[IMG[b], p % 3, b, :], src).then_inc(s_stack[p % 3], 16)
                    shifted = signs[IMG[b], p, 1:PADDED].rearrange("q (o n) -> q o n", o=1)\
                        .broadcast_to([64, 2, PADDED - 1])
                    dst = stack[IMG[1 - b], p % 3, b, :].rearrange("q (o n) -> q o n", o=2)[:, :, 0:PADDED - 1]
                    sp.dma_start(dst, shifted).then_inc(s_stack[p % 3], 16)

            def split_pair(p):
                sp.wait_ge(s_ul, p + 1)
                for b in range(2):
                    sp.dma_start(split[IMG[b], p, b, :], uh[IMG[b], :]).then_inc(s_split[p], 16)
                    sp.dma_start(split[IMG[1 - b], p, b, :], ul[IMG[b], :]).then_inc(s_split[p], 16)

            for s in range(PAIRS + 5):
                if s < PAIRS:
                    stack_pair(s)
                    if s + 4 < PAIRS:
                        sp.dma_start(xs[:, s + 4, :], x_pairs[s + 4]).then_inc(s_x[s + 4], 16)
                if s >= 5:
                    split_pair(s - 5)
            for p in range(PAIRS):
                sp.wait_ge(s_o, p + 1)
                sp.dma_start(out_pairs[p], xs[:, p, :]).then_inc(s_out, 16)
            sp.wait_ge(s_out, 16 * PAIRS)

        @block.tensor
        def _(pe):
            def centre(p):
                pe.wait_ge(s_x[p], 16)
                if p == 0:
                    pe.wait_ge(s_const, 32)
                else:
                    pe.wait_ge(s_keep, p)
                    pe.wait_ge(s_sign, p)
                for h in range(2):
                    mm = nc.tensor.matmul(cen_ps[:, h, :], c32[:, C_CENTER:C_CENTER + 128],
                                          xs[:, p, h * HALF:(h + 1) * HALF], start=True, stop=True)
                mm.then_inc(s_cen, 1)

            def turn_conv_weights():
                pe.wait_ge(s_cw_ord, 6)
                tr = misc_ps[:, 0:384].bitcast(F16).rearrange("q (n o) -> q n o", o=64)
                n = 0
                for b in range(2):
                    for r in range(3):
                        for h in range(2):
                            mm = nc.tensor.transpose(tr[:, n, :], cwo[:, b, r, h, :, :].rearrange("o t i -> o (t i)"),
                                                     c16[0:64, C_ID16:C_ID16 + 64])
                            n += 1
                mm.then_inc(s_cw_tr, 1)

            def convolve(p):
                pe.wait_ge(s_stack[p % 3], 64 * (p // 3 + 1))
                if p == 0:
                    pe.wait_ge(s_cw_done, 1)
                else:
                    pe.wait_ge(s_xc, p)
                for h in range(2):
                    for r in range(3):
                        for t in range(2):
                            for b in range(2):
                                rows = padded(stack[:, p % 3, b, t * PADDED:(t + 1) * PADDED])
                                at = ROWS_HALF * h + r
                                mm = nc.tensor.matmul(conv_ps[IMG[b], h, :], cwT[:, b, r, t, :],
                                                      rows[:, at:at + ROWS_HALF, t:t + W],
                                                      start=(r == 0 and t == 0), stop=(r == 2 and t == 1),
                                                      skip_group_check=True)
                    mm.then_inc(s_conv, 1)

            def centre_conv(p):
                for h in range(2):
                    pe.wait_ge(s_c16, 2 * p + h + 1)
                    mm = nc.tensor.matmul(conv_ps[:, h, :], c16[:, C_NEGMEAN:C_NEGMEAN + 128],
                                          conv16[:, p, h * HALF:(h + 1) * HALF], start=False, stop=True,
                                          skip_group_check=True)
                mm.then_inc(s_cc, 1)

            def variances(n):
                pe.wait_ge(s_sq, n + 1)
                if n >= 1:
                    pe.wait_ge(s_vt, n)
                for j in range(4):
                    mm = nc.tensor.matmul(var_ps[32 * j:32 * j + 32, :], c32[:, C_SUM:C_SUM + 32],
                                          sq[:, j * QUARTER:(j + 1) * QUARTER], start=True, stop=True)
                mm.then_inc(s_var, 1)

            def spread(p):
                pe.wait_ge(s_rt, p + 1)
                if p >= 1:
                    pe.wait_ge(s_u, p)
                for j in range(4):
                    mm = nc.tensor.matmul(spread_ps[:, j // 2, (j % 2) * QUARTER:(j % 2 + 1) * QUARTER],
                                          c16[:, C_SPREAD + 128 * j:C_SPREAD + 128 * (j + 1)], rstd_t[:],
                                          start=True, stop=True)
                mm.then_inc(s_sp, 1)

            for p in range(3):
                centre(p)
                if p == 0:
                    turn_conv_weights()
            for p in range(PAIRS):
                convolve(p)
                if p >= 2:
                    spread(p - 2)
                if p >= 1:
                    variances(p - 1)
                if p + 3 < PAIRS:
                    centre(p + 3)
                centre_conv(p)
            spread(PAIRS - 2)
            variances(PAIRS - 1)
            spread(PAIRS - 1)

            pe.wait_ge(s_ublk, 3)
            nc.tensor.matmul(misc_ps[0:N_IMG, 0:8], ublk[:].rearrange("q b n -> q (b n)"), wr[:],
                             start=True, stop=True).then_inc(s_route_pe, 1)
            pe.wait_ge(s_route_dve, 4)
            nc.tensor.matmul(misc_ps[0:N_IMG, 8:16], c32[0:N_IMG, C_ONES:C_ONES + N_IMG], rt[:, 3, :],
                             start=True, stop=True).then_inc(s_route_pe, 1)
            pe.wait_ge(s_route_dve, ROUTE_DIAG)
            nc.tensor.matmul(misc_ps[:, 16:80], c32[0:N_IMG, C_ONES:C_ONES + 128],
                             diag[:].rearrange("q a k n -> q (a k n)"), start=True, stop=True).then_inc(s_route_pe, 1)
            pe.wait_ge(s_route_dve, ROUTE_HOT)
            nc.tensor.matmul(misc_ps[:, 80:112], b1f[:], hot[:], start=True, stop=True).then_inc(s_route_pe, 1)
            pe.wait_ge(s_route_dve, ROUTE_DENSE)
            for b in range(2):
                mm = nc.tensor.matmul(misc_ps[IMG[b], 112:120], b2f[:], wden[:, 0, b * PAIRS:(b + 1) * PAIRS],
                                      start=True, stop=True)
            mm.then_inc(s_route_pe, 1)

            def up(p, k, b):
                u = 2 * (2 * p + k) + b
                e = pe.value_load(offs[0:1, 0, k * 16 + b * PAIRS + p:k * 16 + b * PAIRS + p + 1],
                                  min_val=0, max_val=(EXPERTS - 1) * 2 * FFN)
                if u < 2:
                    pe.wait_ge(s_split[p], 64)
                elif k == 0:
                    pe.wait_ge(s_split[p], 64)
                if u >= 2:
                    pe.wait_ge(s_gelu, u - 1)
                table = w1s[:].rearrange("q e s f -> q (e s f)")
                for h in range(2):
                    for part in range(2):
                        mm = nc.tensor.matmul(hid_ps[b][:, h, :], table[:, bass.ds(e + part * FFN, FFN)],
                                              split[:, p, b, h * HALF:(h + 1) * HALF],
                                              start=(part == 0), stop=(part == 1))
                mm.then_inc(s_up, 1)

            def down(p, k):
                pe.wait_ge(s_gelu, 2 * (2 * p + k) + 2)
                pe.wait_ge(s_w2s, 4 * p + 2 * k + 2)
                if k == 0 and p >= 1:
                    pe.wait_ge(s_z, p)
                for h in range(2):
                    for b in range(2):
                        mm = nc.tensor.matmul(y_ps[IMG[b], h, :], w2sel[:, k, b, p, :],
                                              hid[:, k, b, h * HALF:(h + 1) * HALF],
                                              start=(k == 0), stop=(k == 1), skip_group_check=True)
                mm.then_inc(s_down, 1)

            def spread_out(p, h):
                if h == 0:
                    pe.wait_ge(s_rt, PAIRS + p + 1)
                if p == 0 and h == 0:
                    pe.wait_ge(s_route_dve, ROUTE_LAST)
                if p + h >= 1:
                    pe.wait_ge(s_zr, 2 * p + h)
                for j in range(2):
                    q = 2 * h + j
                    mm = nc.tensor.matmul(spread2_ps[:, j * QUARTER:(j + 1) * QUARTER],
                                          c16[:, C_SPREAD + 128 * q:C_SPREAD + 128 * (q + 1)], rstd_t[:],
                                          start=True, stop=True)
                mm.then_inc(s_sp2, 1)

            pe.wait_ge(s_w1l, 1)
            pe.wait_ge(s_route_dve, ROUTE_OFFS)
            for p in range(PAIRS):
                up(p, 0, 0)
                up(p, 0, 1)
                if p >= 2:
                    spread_out(p - 2, 0)
                if p >= 1:
                    down(p - 1, 1)
                if p >= 2:
                    spread_out(p - 2, 1)
                up(p, 1, 0)
                up(p, 1, 1)
                down(p, 0)
                if p >= 1:
                    variances(PAIRS + p - 1)
            down(PAIRS - 1, 1)
            spread_out(PAIRS - 2, 0)
            spread_out(PAIRS - 2, 1)
            variances(2 * PAIRS - 1)
            spread_out(PAIRS - 1, 0)
            spread_out(PAIRS - 1, 1)

        @block.scalar
        def _(act):
            act.wait_ge(s_cw, 16)
            nc.scalar.activation(cws[:], cw[:], ACT.Sign).then_inc(s_cw_sign, 1)

            def signs_of(p):
                act.wait_ge(s_cen, p + 1)
                act.wait_ge(s_zero, 1 + ZERO_OF[p])
                grid = padded(signs[:, p, 0:PADDED])[:, 1:1 + H, 1:1 + W]
                nc.scalar.activation(grid, cen_ps.rearrange("q h (r c) -> q (h r) c", c=W), ACT.Sign,
                                     saturate=False).then_inc(s_sign, 1)
                nc.scalar.activation(us[:, p, :], cen_ps.rearrange("q h n -> q (h n)"), ACT.Copy).then_inc(s_keep, 1)

            def keep_conv(p):
                for h in range(2):
                    act.wait_ge(s_conv, 2 * p + h + 1)
                    nc.scalar.activation(conv16[:, p, h * HALF:(h + 1) * HALF], conv_ps[:, h, :],
                                         ACT.Copy).then_inc(s_c16, 1)

            def square(n):
                act.wait_ge(s_xc if n < PAIRS else s_z, n % PAIRS + 1)
                if n >= 1:
                    act.wait_ge(s_var, n)
                nc.scalar.activation(sq[:], us[:, n % PAIRS, :], ACT.Square).then_inc(s_sq, 1)

            def token_high(p):
                act.wait_ge(s_u, p + 1)
                if p >= 1:
                    act.wait_ge(s_split[p - 1], 64)
                nc.scalar.activation(uh[:], us[:, p, :], ACT.Copy).then_inc(s_uh, 1)

            for p in range(3):
                signs_of(p)
            act.wait_ge(s_w1, 32)
            nc.scalar.activation(w1s[:, :, 0, :], w1f[:], ACT.Copy, scale=W1_SCALE).then_inc(s_w1h, 1)
            for p in range(PAIRS):
                if p >= 1:
                    square(p - 1)
                keep_conv(p)
                if p + 3 < PAIRS:
                    signs_of(p + 3)
                if p >= 2:
                    token_high(p - 2)
            square(PAIRS - 1)
            token_high(PAIRS - 2)
            token_high(PAIRS - 1)

            act.wait_ge(s_route_dve, 2)
            nc.scalar.activation(rt[:, 1, :], rt[:, 0, :], ACT.Exp, bias=rc[:, 0:1],
                                 accum_out=rc[:, 1:2]).then_inc(s_route_act, 1)
            act.wait_ge(s_route_dve, 8)
            nc.scalar.activation(rt[:, 5, :], rt[:, 4, :], ACT.Exp, bias=rc[:, 4:5],
                                 accum_out=rc[:, 5:6]).then_inc(s_route_act, 1)
            act.wait_ge(s_route_dve, ROUTE_GAP)
            nc.scalar.activation(rc[:, 12:13], rc[:, 11:12], ACT.Exp).then_inc(s_route_act, 1)

            def gelu(p, k, b):
                u = 2 * (2 * p + k) + b
                act.wait_ge(s_up, u + 1)
                if u == 0:
                    act.wait_ge(s_route_dve, ROUTE_B1)
                if p >= 1:
                    act.wait_ge(s_down, 2 * p + k - 1)
                col = k * 16 + b * PAIRS + p
                nc.scalar.activation(hid[:, k, b, :], hid_ps[b].rearrange("q h n -> q (h n)"), ACT.Gelu,
                                     bias=b1sel[:, col:col + 1], scale=1 / W1_SCALE).then_inc(s_gelu, 1)

            for p in range(PAIRS):
                gelu(p, 0, 0)
                gelu(p, 0, 1)
                gelu(p, 1, 0)
                if p >= 1:
                    square(PAIRS + p - 1)
                gelu(p, 1, 1)
            square(2 * PAIRS - 1)

        @block.gpsimd
        def _(pool):
            words = signs[:].rearrange("q p n -> q (p n)").bitcast(F32)
            zw = REGIONS // 4
            nc.gpsimd.memset(words[:, 0:zw], 0.0).then_inc(s_zero, 1)
            nc.gpsimd.memset(words[:, zw:4 * zw], 0.0).then_inc(s_zero, 1)
            nc.gpsimd.memset(neg_half[:], -0.5).then_inc(s_zero, 1)
            nc.gpsimd.memset(words[:, 4 * zw:], 0.0).then_inc(s_zero, 1)

            def product(p):
                pool.wait_ge(s_edge, p + 1)
                nc.gpsimd.tensor_tensor(out=signs[:, p, PADDED + 1:2 * PADDED - 1], in0=edge[:, 1:PADDED - 1],
                                        in1=signs[:, p, 1:PADDED - 1], op=ALU.mult, saturate=False).then_inc(s_prod, 1)

            def rstd(n):
                pool.wait_ge(s_vc, n + 1)
                if n >= 1:
                    pool.wait_ge(s_rl, n)
                nc.gpsimd.tensor_tensor(out=rstd_c[:].rearrange("q a b -> q (a b)"),
                                        in0=var_c[:].rearrange("q a b -> q (a b)"), in1=neg_half[:],
                                        op=ALU.pow).then_inc(s_pow, 1)

            def token_low(p):
                pool.wait_ge(s_uh, p + 1)
                nc.gpsimd.tensor_tensor(out=ul[:], in0=us[:, p, :], in1=uh[:], op=ALU.subtract).then_inc(s_ul, 1)

            pool.wait_ge(s_zero, 4)
            for p in range(3):
                product(p)
            for p in range(PAIRS):
                if p >= 1:
                    rstd(p - 1)
                if p + 3 < PAIRS:
                    product(p + 3)
                if p >= 2:
                    token_low(p - 2)
            rstd(PAIRS - 1)
            token_low(PAIRS - 2)
            token_low(PAIRS - 1)

            table = w2f[:].rearrange("q e d -> q (e d)")

            def select_w2(p):
                for k in range(2):
                    for b in range(2):
                        col = k * 16 + b * PAIRS + p
                        e = pool.value_load(offs[0:1, 1, col:col + 1], min_val=0, max_val=(EXPERTS - 1) * CH)
                        nc.gpsimd.tensor_tensor(out=w2sel[:, k, b, p, :], in0=table[:, bass.ds(e, CH)],
                                                in1=picks[:, 0, k, b * PAIRS + p:b * PAIRS + p + 1].broadcast_to([128, CH]),
                                                op=ALU.mult).then_inc(s_w2s, 1)

            pool.wait_ge(s_route_dve, ROUTE_OFFS)
            pool.wait_ge(s_w2c, 4)
            select_w2(0)
            for p in range(PAIRS):
                if p + 1 < PAIRS:
                    select_w2(p + 1)
                nc.gpsimd.tensor_tensor(out=xs[:, p, :], in0=xs[:, p, :], in1=conv16[:, p, :],
                                        op=ALU.add).then_inc(s_res, 1)
                if p >= 1:
                    rstd(PAIRS + p - 1)
            rstd(2 * PAIRS - 1)

        @block.vector
        def _(dve):
            nc.vector.memset(rstd_s[:], 0.0).then_inc(s_zero_v, 1)
            nc.vector.memset(ublk[:], 0.0).then_inc(s_ublk, 1)

            def edges(p):
                dve.wait_ge(s_sign, p + 1)
                if p >= 1:
                    dve.wait_ge(s_prod, p)
                nc.vector.tensor_tensor(out=edge[:, 1:PADDED - 1], in0=signs[:, p, 0:PADDED - 2],
                                        in1=signs[:, p, 2:PADDED], op=ALU.mult).then_inc(s_edge, 1)

            def order_conv_weights():
                dve.wait_ge(s_cw_sign, 1)
                nc.vector.tensor_tensor(out=cwp[:], in0=cws[:, :, 0, :], in1=cws[:, :, 1, :], op=ALU.mult).then_inc(s_cw_prep, 1)
                dve.wait_ge(s_cw_prep, 1)
                nc.vector.scalar_tensor_tensor(out=cwo[:, 0, :, 1, 0, :], in0=cwp[:], scalar=-0.5, in1=cws[:, :, 2, :],
                                               op0=ALU.mult, op1=ALU.mult).then_inc(s_cw_ord, 1)
                nc.vector.scalar_tensor_tensor(out=cwo[:, 1, :, 1, 1, :], in0=cwp[:], scalar=-0.5, in1=cws[:, :, 2, :],
                                               op0=ALU.mult, op1=ALU.mult).then_inc(s_cw_ord, 1)
                nc.vector.tensor_scalar(cwo[:, 0, :, 0, :, :], cws[:, :, 0:2, :], 0.5, None, ALU.mult).then_inc(s_cw_ord, 1)
                for t in range(2):
                    i = nc.vector.tensor_scalar(cwo[:, 1, :, 0, t, :], cws[:, :, 1 - t, :], 0.5, None, ALU.mult)
                    if t == 1:
                        i.then_inc(s_cw_ord, 1)
                nc.vector.tensor_scalar(cwo[:, 0, :, 1, 1, :], cws[:, :, 2, :], 0.5, None, ALU.mult).then_inc(s_cw_ord, 1)
                nc.vector.tensor_scalar(cwo[:, 1, :, 1, 0, :], cws[:, :, 2, :], 0.5, None, ALU.mult).then_inc(s_cw_ord, 1)
                dve.wait_ge(s_cw_tr, 1)
                nc.vector.tensor_copy(cwT[:].rearrange("q b r t o -> q (b r t o)"),
                                      misc_ps[:, 0:384].bitcast(F16)).then_inc(s_cw_done, 1)

            def expert_weights():
                dve.wait_ge(s_w1h, 1)
                nc.vector.scalar_tensor_tensor(out=w1s[:, :, 1, :], in0=w1f[:], scalar=W1_SCALE, in1=w1s[:, :, 0, :],
                                               op0=ALU.mult, op1=ALU.subtract).then_inc(s_w1l, 1)
                dve.wait_ge(s_w, 16 * 10)
                nc.vector.tensor_reduce(w2m[:], w2f[:], AX.X, ALU.add).then_inc(s_w2c, 1)
                nc.vector.tensor_reduce(b2m[:], b2f[:], AX.X, ALU.add).then_inc(s_w2c, 1)
                dve.wait_ge(s_w2c, 2)
                mean = w2m[:].rearrange("q (e o) -> q e o", o=1).broadcast_to([128, EXPERTS, CH])
                nc.vector.scalar_tensor_tensor(out=w2f[:], in0=mean, scalar=-1.0 / CH, in1=w2f[:],
                                               op0=ALU.mult, op1=ALU.add).then_inc(s_w2c, 1)
                nc.vector.scalar_tensor_tensor(out=b2f[:], in0=b2m[:].broadcast_to([EXPERTS, CH]), scalar=-1.0 / CH,
                                               in1=b2f[:], op0=ALU.mult, op1=ALU.add).then_inc(s_w2c, 1)

            def compact(n):
                dve.wait_ge(s_var, n + 1)
                if n >= 1:
                    dve.wait_ge(s_vc, n)
                nc.vector.transpose(var_t[:], var_ps).then_inc(s_vt, 1)
                dve.wait_ge(s_vt, n + 1)
                if n >= 1:
                    dve.wait_ge(s_pow, n)
                nc.vector.tensor_scalar(var_c[:], var_t[:].rearrange("q (a c) -> q a c", c=32)[:, :, 0:2],
                                        RSTD_SCALE ** -2, EPS_LN * RSTD_SCALE ** -2, ALU.mult, ALU.add).then_inc(s_vc, 1)

            def rows(n):
                dve.wait_ge(s_pow, n + 1)
                if n == 0:
                    dve.wait_ge(s_zero_v, 1)
                else:
                    dve.wait_ge(s_rt, n)
                nc.vector.tensor_copy(rstd_s[:, :, 0:2], rstd_c[:]).then_inc(s_rh, 1)
                dve.wait_ge(s_rh, n + 1)
                nc.vector.tensor_tensor(out=rstd_s[:, :, 2:4], in0=rstd_c[:], in1=rstd_s[:, :, 0:2],
                                        op=ALU.subtract).then_inc(s_rl, 1)
                dve.wait_ge(s_rl, n + 1)
                if 1 <= n < PAIRS + 1:
                    dve.wait_ge(s_sp, min(n, PAIRS))
                elif n > PAIRS:
                    dve.wait_ge(s_sp2, 2 * (n - PAIRS))
                nc.vector.transpose(rstd_t[:], rstd_s[:].rearrange("q a c -> q (a c)")).then_inc(s_rt, 1)

            def residual(p):
                dve.wait_ge(s_cc, p + 1)
                nc.vector.tensor_tensor(out=us[:, p, :], in0=us[:, p, :], in1=conv_ps.rearrange("q h n -> q (h n)"),
                                        op=ALU.add).then_inc(s_xc, 1)

            def tokens(p):
                dve.wait_ge(s_sp, p + 1)
                nc.vector.scalar_tensor_tensor(out=us[:, p, :], in0=us[:, p, :], scalar=1.0,
                                               in1=spread_ps.rearrange("q h n -> q (h n)"), op0=ALU.mult, op1=ALU.mult,
                                               accum_out=usum[:, p:p + 1]).then_inc(s_u, 1)

            order_conv_weights()
            for p in range(3):
                edges(p)
            expert_weights()
            for p in range(PAIRS):
                if p >= 2:
                    tokens(p - 2)
                if p >= 1:
                    compact(p - 1)
                residual(p)
                if p >= 1:
                    rows(p - 1)
                if p + 3 < PAIRS:
                    edges(p + 3)
            tokens(PAIRS - 2)
            compact(PAIRS - 1)
            rows(PAIRS - 1)
            tokens(PAIRS - 1)

            dve.wait_ge(s_u, PAIRS)
            dve.wait_ge(s_ublk, 1)
            nc.vector.tensor_copy(ublk[LO, 0, :], usum[LO, :]).then_inc(s_ublk, 1)
            nc.vector.tensor_copy(ublk[HI, 1, :], usum[HI, :]).then_inc(s_ublk, 1)
            steps = [0]

            def step(i):
                steps[0] += 1
                i.then_inc(s_route_dve, 1)
                dve.wait_ge(s_route_dve, steps[0])

            V = nc.vector
            dve.wait_ge(s_route_pe, 1)
            step(V.scalar_tensor_tensor(out=rt[:, 0, :], in0=misc_ps[0:16, 0:8], scalar=1.0 / TOK, in1=brs[:],
                                        op0=ALU.mult, op1=ALU.add))
            step(V.tensor_reduce(rc[:, 0:1], rt[:, 0, :], AX.X, ALU.max, negate=True))
            dve.wait_ge(s_route_act, 1)
            step(V.reciprocal(rc[:, 2:3], rc[:, 1:2]))
            step(V.tensor_scalar(rt[:, 3, :], rt[:, 1, :], rc[:, 2:3], None, ALU.mult))
            dve.wait_ge(s_route_pe, 2)
            step(V.reciprocal(rt[:, 2, :], misc_ps[0:16, 8:16]))
            step(V.tensor_scalar(rt[:, 2, :], rt[:, 2, :], CAPACITY / TOK, 1.0, ALU.mult, ALU.min))
            step(V.tensor_tensor(out=rt[:, 4, :], in0=rt[:, 3, :], in1=rt[:, 2, :], op=ALU.mult))
            step(V.tensor_reduce(rc[:, 4:5], rt[:, 4, :], AX.X, ALU.max, negate=True))
            dve.wait_ge(s_route_act, 2)
            step(V.reciprocal(rc[:, 6:7], rc[:, 5:6]))
            step(V.tensor_scalar(rt[:, 6, :], rt[:, 5, :], rc[:, 6:7], None, ALU.mult))
            iota = c32[0:16, C_IOTA8:C_IOTA8 + 8]
            for k in range(2):
                v = rt[:, 6 + k, :]
                step(V.tensor_reduce(rc[:, 7 + k:8 + k], v, AX.X, ALU.max))
                step(V.scalar_tensor_tensor(out=rt[:, 8, :], in0=v, scalar=rc[:, 7 + k:8 + k], in1=iota,
                                            op0=ALU.is_equal, op1=ALU.mult))
                step(V.tensor_reduce(rc[:, 9 + k:10 + k], rt[:, 8, :], AX.X, ALU.min))
                if k == 0:
                    step(V.tensor_scalar(rt[:, 9, :], iota, rc[:, 9:10], -10.0, ALU.is_equal, ALU.mult))
                    step(V.tensor_tensor(out=rt[:, 7, :], in0=rt[:, 6, :], in1=rt[:, 9, :], op=ALU.add))
            step(V.tensor_tensor(out=rc[:, 11:12], in0=rc[:, 8:9], in1=rc[:, 7:8], op=ALU.subtract))
            assert steps[0] == ROUTE_GAP
            dve.wait_ge(s_route_act, 3)
            step(V.tensor_scalar(rc[:, 13:14], rc[:, 12:13], 1.0, None, ALU.add))
            step(V.reciprocal(rc[:, 14:15], rc[:, 13:14]))
            step(V.tensor_tensor(out=rc[:, 15:16], in0=rc[:, 14:15], in1=rc[:, 12:13], op=ALU.mult))
            eye = c32[0:16, C_EYE:C_EYE + 16]
            for k in range(2):
                step(V.tensor_scalar(diag[:, 0, k, :], eye, rc[:, 14 + k:15 + k], None, ALU.mult))
                step(V.tensor_scalar(diag[:, 1, k, :], eye, rc[:, 9 + k:10 + k], None, ALU.mult))
            assert steps[0] == ROUTE_DIAG
            dve.wait_ge(s_route_pe, 3)
            pk = misc_ps[:, 16:80].rearrange("q (a n) -> q a n", a=2)
            step(V.tensor_scalar(offs[0:1, 0, :], pk[0:1, 1, :], 8.0, float(2 * FFN), ALU.add, ALU.mult))
            step(V.tensor_scalar(offs[0:1, 1, :], pk[0:1, 1, :], 8.0, float(CH), ALU.add, ALU.mult))
            step(V.tensor_copy(picks[:].rearrange("q a k n -> q (a k n)"), misc_ps[:, 16:80]))
            assert steps[0] == ROUTE_OFFS
            pks = picks[0:8, 1, :, :].rearrange("q k n -> q (k n)")
            step(V.tensor_scalar(hot[:], pks, 8.0, c32[0:8, C_PART:C_PART + 1], ALU.add, ALU.is_equal))
            assert steps[0] == ROUTE_HOT
            step(V.tensor_tensor(out=wden[:].rearrange("q k n -> q (k n)"), in0=hot[:],
                                 in1=picks[0:8, 0, :, :].rearrange("q k n -> q (k n)"), op=ALU.mult))
            step(V.tensor_tensor(out=wden[:, 0, :], in0=wden[:, 0, :], in1=wden[:, 1, :], op=ALU.add))
            assert steps[0] == ROUTE_DENSE
            dve.wait_ge(s_route_pe, 5)
            step(V.tensor_copy(b1sel[:], misc_ps[:, 80:112]))
            assert steps[0] == ROUTE_B1
            step(V.tensor_copy(b2sel[:], misc_ps[:, 112:120]))
            assert steps[0] == ROUTE_LAST

            def mixture(p):
                dve.wait_ge(s_down, 2 * p + 2)
                nc.vector.scalar_tensor_tensor(out=us[:, p, :], in0=y_ps.rearrange("q h n -> q (h n)"),
                                               scalar=b2sel[:, p:p + 1], in1=us[:, p, :],
                                               op0=ALU.add, op1=ALU.add).then_inc(s_z, 1)

            def normalise(p, h):
                dve.wait_ge(s_sp2, 2 * p + h + 1)
                half = us[:, p, h * HALF:(h + 1) * HALF]
                nc.vector.scalar_tensor_tensor(out=half, in0=half, scalar=gam[:], in1=spread2_ps,
                                               op0=ALU.mult, op1=ALU.mult).then_inc(s_zr, 1)

            def output(p):
                dve.wait_ge(s_zr, 2 * p + 2)
                dve.wait_ge(s_res, p + 1)
                nc.vector.scalar_tensor_tensor(out=xs[:, p, :], in0=us[:, p, :], scalar=bet[:], in1=xs[:, p, :],
                                               op0=ALU.add, op1=ALU.add).then_inc(s_o, 1)

            for p in range(PAIRS):
                if p >= 2:
                    normalise(p - 2, 0)
                if p >= 1:
                    mixture(p - 1)
                if p >= 2:
                    normalise(p - 2, 1)
                    output(p - 2)
                if p >= 1:
                    compact(PAIRS + p - 1)
                    rows(PAIRS + p - 1)
            mixture(PAIRS - 1)
            normalise(PAIRS - 2, 0)
            normalise(PAIRS - 2, 1)
            compact(2 * PAIRS - 1)
            output(PAIRS - 2)
            rows(2 * PAIRS - 1)
            normalise(PAIRS - 1, 0)
            normalise(PAIRS - 1, 1)
            output(PAIRS - 1)


_INS = ["x", "L0_conv_weight", "L0_ffn_Wr", "L0_ffn_br", "L0_ffn_W1", "L0_ffn_b1", "L0_ffn_W2", "L0_ffn_b2",
        "L0_ffn_gamma", "L0_ffn_beta"]


def kernel(**inputs):
    import concourse.bacc as _bacc
    from concourse import mybir as _mybir
    from concourse.bass_utils import run_bass_kernel_spmd as _run

    nc = _bacc.Bacc("TRN2", target_bir_lowering=False, num_devices=1)
    arrays, args = {}, []
    c32, c16 = constants()
    for name, a in [(n, np.ascontiguousarray(inputs[n])) for n in _INS] + [("const32", c32), ("const16", c16)]:
        arrays[f"in_{name}"] = a
        args.append(nc.dram_tensor(f"in_{name}", a.shape, _mybir.dt.from_np(a.dtype), kind="ExternalInput").ap())
    args.append(nc.dram_tensor("out_0", (N_IMG, CH, H, W), _mybir.dt.float32, kind="ExternalOutput").ap())
    metaformer(nc, *args)
    return _run(nc, [arrays], core_ids=[0]).results[0]["out_0"]
```

```python
from contextlib import ExitStack

import numpy as np

import concourse.bass as bass
from concourse import mybir

N_IMG, CH, H, W = 16, 64, 32, 32
TOK = H * W
PAIRS = N_IMG // 2
EXPERTS, FFN = 8, 128
HALF = TOK // 2
ROWS_HALF = H // 2
PW = W + 2
PADDED = (H + 2) * PW
REGIONS = 2 * PADDED
QUARTER = TOK // 4
EPS_LN = 1e-5
CAPACITY = float(-(-N_IMG * TOK * 5 // (4 * EXPERTS)))
RSTD_SCALE = 128.0
W1_SCALE = 64.0

C_CENTER, C_SUM, C_IOTA8, C_PART, C_EYE, C_ONES = 0, 128, 160, 168, 169, 185
C_LOAD = C_ONES + 128
C32 = C_LOAD + 16
C_NEGMEAN, C_SPREAD, C_ID16 = 0, 128, 640
C16 = C_ID16 + 64


WIDE, GROUPS = 2, PAIRS // 2
MAGIC = float(0x5F3759DF)
NEWTON_STEPS = 12
ZERO_OF = [0, 1, 1, 1, 2, 2, 2, 2]


def constants():
    c = np.zeros((128, C32), np.float32)
    for b in (0, 64):
        c[b:b + 64, C_CENTER + b:C_CENTER + b + 64] = np.eye(64) - 1.0 / CH
        c[b:b + 64, C_SUM + b // 64] = 1.0 / CH
    c[:, C_IOTA8:C_IOTA8 + 8] = np.arange(8) - 8
    c[:, C_PART] = np.arange(128)
    c[0:16, C_EYE:C_EYE + 16] = np.eye(16)
    c[:, C_ONES:C_ONES + 128] = 1.0
    c[:, C_LOAD:C_LOAD + 16] = TOK / CAPACITY
    d = np.zeros((128, C16), np.float16)
    for b in (0, 64):
        d[b:b + 64, C_NEGMEAN + b:C_NEGMEAN + b + 64] = -1.0 / CH
    for j in range(4):
        for b in (0, 1):
            for part in (0, 2):
                d[32 * j + part + b, C_SPREAD + 128 * j + 64 * b:C_SPREAD + 128 * j + 64 * b + 64] = 1 / RSTD_SCALE
    d[0:64, C_ID16:C_ID16 + 64] = np.eye(64)
    return c, d


def metaformer(nc, x, conv_w, Wr, br, W1, b1, W2, b2, gamma, beta, const32, const16, out):
    F32, F16, I32, F8 = mybir.dt.float32, mybir.dt.float16, mybir.dt.int32, mybir.dt.float8e4
    ALU, ACT, AX = mybir.AluOpType, mybir.ActivationFunctionType, mybir.AxisListType
    LO, HI = slice(0, 64), slice(64, 128)
    IMG = (LO, HI)

    x_pairs = x.rearrange("(q b) c h w -> q (b c) (h w)", b=2)
    out_pairs = out.rearrange("(q b) c h w -> q (b c) (h w)", b=2)

    with ExitStack() as ctx:
        def sb(name, shape, dt=F32):
            return ctx.enter_context(nc.sbuf_tensor(name, shape, dt))

        def sem(name):
            return ctx.enter_context(nc.semaphore(name))

        xs = sb("xs", [128, PAIRS, TOK])
        us = sb("us", [128, PAIRS, TOK])
        conv16 = sb("conv16", [128, PAIRS, TOK], F16)
        split = sb("split", [128, PAIRS, 2, TOK], F16)
        signs = sb("signs", [128, PAIRS, REGIONS], F8)
        stack = sb("stack", [128, 3, 2, REGIONS], F8)
        edge = sb("edge", [128, PADDED], F16)
        uh = sb("uh", [128, 2, TOK], F16)
        ul = sb("ul", [128, 2, TOK], F16)
        sq = sb("sq", [128, WIDE, TOK])
        hid = signs[:].rearrange("q p n -> q (p n)").bitcast(F32)[:, 0:4 * TOK]\
            .rearrange("q (k b n) -> q k b n", k=2, b=2)
        var_t = sb("var_t", [128, HALF])
        stat = sb("stat", [128, 4, 16, 2])
        rstd_s = sb("rstd_s", [128, 16, 32], F16)
        rstd_t = sb("rstd_t", [128, HALF], F16)
        c32 = sb("c32", [128, C32])
        c16 = sb("c16", [128, C16], F16)
        cw = sb("cw", [64, 3, 3, 64])
        cws = sb("cws", [64, 3, 3, 64], F16)
        cwp = sb("cwp", [64, 3, 64], F16)
        cwo = sb("cwo", [64, 2, 3, 2, 2, 64], F16)
        cwT = sb("cwT", [128, 2, 3, 2, 64], F16)
        w1f = sb("w1f", [128, EXPERTS, FFN])
        w1s = sb("w1s", [128, EXPERTS, 2, FFN], F16)
        w2f = sb("w2f", [128, EXPERTS, CH])
        w2m = sb("w2m", [128, EXPERTS])
        w2sel = sb("w2sel", [128, 2, 2, PAIRS, CH])
        b1f = sb("b1f", [EXPERTS, FFN])
        b2f = sb("b2f", [EXPERTS, CH])
        b2m = sb("b2m", [EXPERTS, 1])
        wr = sb("wr", [128, EXPERTS])
        brs = sb("brs", [N_IMG, EXPERTS])
        gam = sb("gam", [128, 1])
        bet = sb("bet", [128, 1])
        warm = sb("warm", [128, 1])
        usum = sb("usum", [128, PAIRS])
        ublk = sb("ublk", [128, 2, PAIRS])
        logit, expo, weight = (sb(n, [N_IMG, 2, EXPERTS]) for n in ("logit", "expo", "weight"))
        relief = sb("relief", [N_IMG, EXPERTS])
        neg_top = sb("neg_top", [N_IMG, 3])
        total = sb("total", [N_IMG, 3])
        inverse = sb("inverse", [N_IMG, 3])
        top8 = sb("top8", [N_IMG, 8])
        top8_at = sb("top8_at", [N_IMG, 8], mybir.dt.uint32)
        top_exp = sb("top_exp", [N_IMG, 2])
        diag = sb("diag", [N_IMG, 2, 2, N_IMG])
        picks = sb("picks", [128, 2, 2, N_IMG])
        offs = sb("offs", [1, 2, 32], I32)
        hot = sb("hot", [EXPERTS, 32])
        wden = sb("wden", [EXPERTS, 2, N_IMG])
        b1sel = sb("b1sel", [128, 32])
        b2sel = sb("b2sel", [128, PAIRS])

        ps = ctx.enter_context(nc.psum_tensor("ps", [128, 8, 512], F32))
        cen_ps = [ps[:, b:b + 2, :] for b in (0, 5, 2) + (0,) * (PAIRS - 3)]
        conv_ps = ps[:, 2:4, :]
        var_ps = ps[:, 4, :]
        spread_ps = [ps[:, b:b + 2, :] for b in (5,) * (PAIRS - 1) + (0,)]
        misc_ps = ps[:, 7, :]
        b1_ps = ps[:, 4, 0:32]
        b2_ps = ps[:, 7, 112:112 + PAIRS]
        hid_ps = (ps[:, 0:2, :], ps[:, 2:4, :])
        y_ps = ps[:, 5:7, :]
        spread2_ps = ps[:, 7, :]

        s_x = [sem(f"x_loaded{p}") for p in range(PAIRS)]
        s_c32 = sem("const32_loaded")
        s_c16c = sem("const16_loaded")
        s_cw = sem("conv_weights_loaded")
        s_w1 = sem("w1_loaded")
        s_w = sem("weights_loaded")
        s_zero = sem("zeroed")
        s_zero_v = sem("rstd_columns_zeroed")
        s_cw_sign = sem("conv_weight_signs")
        s_cw_prep = sem("conv_weight_steps")
        s_cw_ord = sem("conv_weights_ordered")
        s_cw_tr = sem("conv_weights_turned")
        s_cw_done = sem("conv_weights_ready")
        s_w1h = sem("w1_high")
        s_w1l = sem("w1_low")
        s_w2c = sem("w2_steps")
        s_cen = sem("centred")
        s_sign = sem("signs_done")
        s_keep = sem("centred_kept")
        s_edge = sem("edge_products")
        s_prod0 = sem("first_products_done")
        s_prod = sem("products_done")
        s_stack = [sem(f"stacked{b}") for b in range(3)]
        s_conv = sem("conv_done")
        s_c16 = sem("conv16_done")
        s_cc = sem("conv_centred")
        s_xc = sem("residual_centred")
        s_sq = sem("squares_done")
        s_var = sem("variances_done")
        s_vt = sem("variances_turned")
        s_vc = sem("variances_compact")
        s_newton = sem("rstd_steps")
        s_rh = sem("rstd_high")
        s_rl = sem("rstd_low")
        s_rt = sem("rstd_rows")
        s_sp = sem("rstd_spread")
        s_u = sem("tokens_done")
        s_uh = sem("token_high")
        s_ul = sem("token_low")
        s_split = [sem(f"token_split{p}") for p in range(PAIRS)]
        s_ublk = sem("token_sums")
        s_route_pe = sem("route_products")
        s_route = {n: sem(n) for n in (
            "logits", "shift1", "weights1", "relief", "scaled", "shift2", "weights2", "top", "negated", "inverse",
            "diagonals", "offsets", "picks", "hot", "dense", "biases")}
        s_route_act = sem("route_scalar_steps")
        s_res = sem("residual_done")
        s_w2s = sem("w2_selected")
        s_up = sem("up_projected")
        s_gelu = sem("hidden_done")
        s_down = sem("down_projected")
        s_z = sem("mixture_centred")
        s_zr = sem("normalised")
        s_sp2 = sem("rstd_spread2")
        s_o = sem("output_done")
        s_out = sem("output_stored")

        block = ctx.enter_context(nc.Block())

        SIGN_AT = lambda b, p: signs[IMG[b], p, :]

        def padded(ap):
            return ap.rearrange("q (r c) -> q r c", c=PW)

        @block.sync
        def _(sp):
            for p in range(4):
                sp.dma_start(xs[:, p, :], x_pairs[p]).then_inc(s_x[p], 16)
            for b in range(2):
                sp.dma_start(w1f[IMG[b], :, :], W1.rearrange("e d f -> d e f")).then_inc(s_w1, 16)
            sp.dma_start(w2f[:], W2.rearrange("e f d -> f e d")).then_inc(s_w, 16)
            sp.dma_start(b1f[:], b1).then_inc(s_w, 16)
            sp.dma_start(b2f[:], b2).then_inc(s_w, 16)
            sp.dma_start(brs[:], br.rearrange("(o e) -> o e", o=1).broadcast_to([N_IMG, EXPERTS])).then_inc(s_w, 16)
            for b in range(2):
                sp.dma_start(wr[IMG[b], :], Wr).then_inc(s_w, 16)
                sp.dma_start(gam[IMG[b], :], gamma.rearrange("(d o) -> d o", o=1)).then_inc(s_w, 16)
                sp.dma_start(bet[IMG[b], :], beta.rearrange("(d o) -> d o", o=1)).then_inc(s_w, 16)

            def stack_signs(p, b):
                shifted = signs[IMG[b], p, 1:PADDED].rearrange("q (o n) -> q o n", o=1)\
                    .broadcast_to([64, 2, PADDED - 1])
                dst = stack[IMG[1 - b], p % 3, b, :].rearrange("q (o n) -> q o n", o=2)[:, :, 0:PADDED - 1]
                sp.dma_start(dst, shifted).then_inc(s_stack[p % 3], 16)

            def stack_own(p, b, regions):
                at = slice(PADDED * regions[0], PADDED * (regions[-1] + 1))
                sp.dma_start(stack[IMG[b], p % 3, b, at], signs[IMG[b], p, at]).then_inc(s_stack[p % 3], 16)

            def stack_pair(p):
                if p == 0:
                    sp.wait_ge(s_sign, 1)
                    for b in range(2):
                        stack_signs(0, b)
                        stack_own(0, b, (0,))
                    sp.wait_ge(s_prod0, 1)
                    for b in range(2):
                        stack_own(0, b, (1,))
                    return
                sp.wait_ge(s_prod, p)
                if p >= 3:
                    sp.wait_ge(s_conv, 2 * (p - 2))
                for b in range(2):
                    stack_own(p, b, (0, 1))
                    stack_signs(p, b)

            def split_pair(p):
                sp.wait_ge(s_ul, p + 1)
                for b in range(2):
                    sp.dma_start(split[IMG[b], p, b, :], uh[IMG[b], p % 2, :]).then_inc(s_split[p], 16)
                    sp.dma_start(split[IMG[1 - b], p, b, :], ul[IMG[b], p % 2, :]).then_inc(s_split[p], 16)

            for s in range(PAIRS + 5):
                if s < PAIRS:
                    stack_pair(s)
                    if s + 4 < PAIRS:
                        sp.dma_start(xs[:, s + 4, :], x_pairs[s + 4]).then_inc(s_x[s + 4], 16)
                if s >= 5:
                    split_pair(s - 5)
            for p in range(PAIRS):
                sp.wait_ge(s_o, p + 1)
                sp.dma_start(out_pairs[p], xs[:, p, :]).then_inc(s_out, 16)
            sp.wait_ge(s_out, 16 * PAIRS)

        @block.tensor
        def _(pe):
            def centre(p, h):
                if h == 0:
                    pe.wait_ge(s_x[p], 16)
                if p == 0:
                    pe.wait_ge(s_c32, 16)
                elif p >= 3 and h == 0:
                    pe.wait_ge(s_keep, p if p > 3 else 1)
                nc.tensor.matmul(cen_ps[p][:, h, :], c32[:, C_CENTER:C_CENTER + 128],
                                 xs[:, p, h * HALF:(h + 1) * HALF], start=True, stop=True).then_inc(s_cen, 1)

            def turn_conv_weights():
                pe.wait_ge(s_cw_ord, 6)
                pe.wait_ge(s_c16c, 16)
                tr = misc_ps[:, 0:384].bitcast(F16).rearrange("q (n o) -> q n o", o=64)
                n = 0
                for b in range(2):
                    for r in range(3):
                        for h in range(2):
                            mm = nc.tensor.transpose(tr[:, n, :], cwo[:, b, r, h, :, :].rearrange("o t i -> o (t i)"),
                                                     c16[0:64, C_ID16:C_ID16 + 64])
                            n += 1
                mm.then_inc(s_cw_tr, 1)

            def convolve(p):
                pe.wait_ge(s_stack[p % 3], 64 * (p // 3 + 1) + (32 if p % 3 == 0 else 0))
                if p == 0:
                    pe.wait_ge(s_cw_done, 1)
                    pe.wait_ge(s_keep, 3)
                for h in range(2):
                    if p >= 1:
                        pe.wait_ge(s_xc, 2 * (p - 1) + h + 1)
                    for r in range(3):
                        for t in range(2):
                            for b in range(2):
                                rows = padded(stack[:, p % 3, b, t * PADDED:(t + 1) * PADDED])
                                at = ROWS_HALF * h + r
                                mm = nc.tensor.matmul(conv_ps[IMG[b], h, :], cwT[:, b, r, t, :],
                                                      rows[:, at:at + ROWS_HALF, t:t + W],
                                                      start=(r == 0 and t == 0), stop=(r == 2 and t == 1),
                                                      skip_group_check=True)
                    mm.then_inc(s_conv, 1)

            def centre_conv(p):
                for h in range(2):
                    pe.wait_ge(s_c16, 2 * p + h + 1)
                    mm = nc.tensor.matmul(conv_ps[:, h, :], c16[:, C_NEGMEAN:C_NEGMEAN + 128],
                                          conv16[:, p, h * HALF:(h + 1) * HALF], start=False, stop=True,
                                          skip_group_check=True)
                    mm.then_inc(s_cc, 1)

            def variances(g):
                pairs = WIDE if g < GROUPS else 1
                pe.wait_ge(s_sq, WIDE * min(g + 1, GROUPS) + max(g + 1 - GROUPS, 0))
                if g >= 1:
                    pe.wait_ge(s_vt, g)
                run = pairs * QUARTER
                flat = sq[:].rearrange("q s n -> q (s n)")
                for j in range(4):
                    mm = nc.tensor.matmul(var_ps[32 * j:32 * j + 32, 0:run], c32[:, C_SUM:C_SUM + 32],
                                          flat[:, j * run:(j + 1) * run], start=True, stop=True)
                mm.then_inc(s_var, 1)

            def spread(p):
                if p % WIDE == 0:
                    pe.wait_ge(s_rt, p // WIDE + 1)
                if 1 <= p < PAIRS - 1:
                    pe.wait_ge(s_u, p)
                for h in range(2):
                    j = 2 * (p % WIDE) + h
                    mm = nc.tensor.matmul(spread_ps[p][:, h, :], c16[:, C_SPREAD + 128 * j:C_SPREAD + 128 * (j + 1)],
                                          rstd_t[:], start=True, stop=True)
                mm.then_inc(s_sp, 1)

            for p in range(3):
                centre(p, 0)
                centre(p, 1)
                if p == 0:
                    turn_conv_weights()
            for p in range(PAIRS):
                convolve(p)
                if p + 3 < PAIRS:
                    centre(p + 3, 0)
                centre_conv(p)
                if p + 3 < PAIRS:
                    centre(p + 3, 1)
                if p >= 3:
                    spread(p - 3)
                if p >= WIDE and p % WIDE == 0:
                    variances(p // WIDE - 1)
            spread(PAIRS - 3)
            variances(GROUPS - 1)
            spread(PAIRS - 2)
            spread(PAIRS - 1)

            pe.wait_ge(s_ublk, 3)
            nc.tensor.matmul(misc_ps[0:N_IMG, 0:8], ublk[:].rearrange("q b n -> q (b n)"), wr[:],
                             start=True, stop=True).then_inc(s_route_pe, 1)
            pe.wait_ge(s_route["weights1"], 1)
            nc.tensor.matmul(misc_ps[0:N_IMG, 8:16], c32[0:N_IMG, C_LOAD:C_LOAD + N_IMG], weight[:, 0, :],
                             start=True, stop=True).then_inc(s_route_pe, 1)
            pe.wait_ge(s_route["diagonals"], 2)
            nc.tensor.matmul(misc_ps[:, 16:80], c32[0:N_IMG, C_ONES:C_ONES + 128],
                             diag[:].rearrange("q a k n -> q (a k n)"), start=True, stop=True).then_inc(s_route_pe, 1)

            def chosen_b1():
                pe.wait_ge(s_route["hot"], 1)
                nc.tensor.matmul(b1_ps, b1f[:], hot[:], start=True, stop=True).then_inc(s_route_pe, 1)

            def chosen_b2():
                pe.wait_ge(s_route["dense"], 2)
                for b in range(2):
                    mm = nc.tensor.matmul(b2_ps[IMG[b], :], b2f[:], wden[:, 0, b * PAIRS:(b + 1) * PAIRS],
                                          start=True, stop=True)
                mm.then_inc(s_route_pe, 1)

            def up(p, k, b):
                u = 2 * (2 * p + k) + b
                e = pe.value_load(offs[0:1, 0, k * 16 + b * PAIRS + p:k * 16 + b * PAIRS + p + 1],
                                  min_val=0, max_val=(EXPERTS - 1) * 2 * FFN)
                if k == 0:
                    pe.wait_ge(s_split[p], 64)
                if u >= 2:
                    pe.wait_ge(s_gelu, u - 1)
                table = w1s[:].rearrange("q e s f -> q (e s f)")
                for h in range(2):
                    for part in range(2):
                        mm = nc.tensor.matmul(hid_ps[b][:, h, :], table[:, bass.ds(e + part * FFN, FFN)],
                                              split[:, p, b, h * HALF:(h + 1) * HALF],
                                              start=(part == 0), stop=(part == 1))
                mm.then_inc(s_up, 1)

            def down(p, k):
                pe.wait_ge(s_gelu, 2 * (2 * p + k) + 2)
                pe.wait_ge(s_w2s, 4 * p + 2 * k + 2)
                if k == 0 and p >= 1:
                    pe.wait_ge(s_z, p)
                for h in range(2):
                    for b in range(2):
                        mm = nc.tensor.matmul(y_ps[IMG[b], h, :], w2sel[:, k, b, p, :],
                                              hid[:, k, b, h * HALF:(h + 1) * HALF],
                                              start=(k == 0), stop=(k == 1), skip_group_check=True)
                mm.then_inc(s_down, 1)

            def spread_out(p, h):
                if h == 0:
                    pe.wait_ge(s_rt, GROUPS + p + 1)
                if p == 0 and h == 0:
                    pe.wait_ge(s_route["biases"], 2)
                if p + h >= 1:
                    pe.wait_ge(s_zr, 2 * p + h)
                for j in range(2):
                    q = 2 * h + j
                    mm = nc.tensor.matmul(spread2_ps[:, j * QUARTER:(j + 1) * QUARTER],
                                          c16[:, C_SPREAD + 128 * q:C_SPREAD + 128 * (q + 1)], rstd_t[:, 0:QUARTER],
                                          start=True, stop=True)
                mm.then_inc(s_sp2, 1)

            pe.wait_ge(s_w1l, 1)
            pe.wait_ge(s_route["offsets"], 1)
            chosen_b1()
            for p in range(PAIRS):
                up(p, 0, 0)
                up(p, 0, 1)
                if p == 0:
                    chosen_b2()
                if p >= 1:
                    down(p - 1, 1)
                up(p, 1, 0)
                if p >= 2:
                    spread_out(p - 2, 0)
                up(p, 1, 1)
                if p >= 2:
                    spread_out(p - 2, 1)
                down(p, 0)
                if p >= 1:
                    variances(GROUPS + p - 1)
            down(PAIRS - 1, 1)
            spread_out(PAIRS - 2, 0)
            spread_out(PAIRS - 2, 1)
            variances(GROUPS + PAIRS - 1)
            spread_out(PAIRS - 1, 0)
            spread_out(PAIRS - 1, 1)

        @block.scalar
        def _(act):
            act.dma_start(c32[:], const32).then_inc(s_c32, 16)
            act.dma_start(cw[:], conv_w).then_inc(s_cw, 16)
            act.dma_start(c16[:], const16).then_inc(s_c16c, 16)
            act.wait_ge(s_cw, 16)
            nc.scalar.activation(cws[:], cw[:], ACT.Sign).then_inc(s_cw_sign, 1)

            def signs_of(p):
                act.wait_ge(s_cen, 2 * p + 2)
                act.wait_ge(s_zero, 1 + ZERO_OF[p])
                grid = padded(signs[:, p, 0:PADDED])[:, 1:1 + H, 1:1 + W]
                nc.scalar.activation(grid, cen_ps[p].rearrange("q h (r c) -> q (h r) c", c=W), ACT.Sign,
                                     saturate=False).then_inc(s_sign, 1)
                nc.scalar.activation(us[:, p, :], cen_ps[p].rearrange("q h n -> q (h n)"), ACT.Copy).then_inc(s_keep, 1)

            def keep_conv(p):
                for h in range(2):
                    act.wait_ge(s_conv, 2 * p + h + 1)
                    nc.scalar.activation(conv16[:, p, h * HALF:(h + 1) * HALF], conv_ps[:, h, :],
                                         ACT.Copy).then_inc(s_c16, 1)

            def square(n):
                if n < PAIRS:
                    act.wait_ge(s_xc, 2 * n + 2)
                else:
                    act.wait_ge(s_z, n - PAIRS + 1)
                slot = n % WIDE if n < PAIRS else 0
                if n >= PAIRS:
                    act.wait_ge(s_var, GROUPS + n - PAIRS)
                elif n >= WIDE:
                    act.wait_ge(s_var, n // WIDE)
                nc.scalar.activation(sq[:, slot, :], us[:, n % PAIRS, :], ACT.Square).then_inc(s_sq, 1)

            def token_high(p):
                act.wait_ge(s_u, p + 1)
                if p >= 2:
                    act.wait_ge(s_split[p - 2], 64)
                nc.scalar.activation(uh[:, p % 2, :], us[:, p, :], ACT.Copy).then_inc(s_uh, 1)

            for p in range(3):
                signs_of(p)
            act.wait_ge(s_w1, 32)
            nc.scalar.activation(w1s[:, :, 0, :], w1f[:], ACT.Copy, scale=W1_SCALE).then_inc(s_w1h, 1)
            for p in range(PAIRS):
                if p >= 1:
                    square(p - 1)
                keep_conv(p)
                if p + 3 < PAIRS:
                    signs_of(p + 3)
                if p >= 3:
                    token_high(p - 3)
            square(PAIRS - 1)
            for p in range(PAIRS - 3, PAIRS):
                token_high(p)

            for n, (source, result) in enumerate(((logit[:, 0, :], expo[:, 0, :]), (logit[:, 1, :], expo[:, 1, :]),
                                                  (top8[:, 0:2], top_exp[:]))):
                if n < 2:
                    act.wait_ge(s_route[f"shift{n + 1}"], 1)
                else:
                    act.wait_ge(s_route["negated"], 1)
                    act.wait_ge(s_route["top"], 1)
                nc.scalar.activation(result, source, ACT.Exp, bias=neg_top[:, n:n + 1],
                                     accum_out=total[:, n:n + 1]).then_inc(s_route_act, 1)

            nc.scalar.activation(warm[:], c32[:, C_ONES:C_ONES + 1], ACT.Gelu)

            def gelu(p, k, b):
                u = 2 * (2 * p + k) + b
                act.wait_ge(s_up, u + 1)
                if u == 0:
                    act.wait_ge(s_route["biases"], 1)
                if p >= 1:
                    act.wait_ge(s_down, 2 * p + k - 1)
                col = k * 16 + b * PAIRS + p
                nc.scalar.activation(hid[:, k, b, :], hid_ps[b].rearrange("q h n -> q (h n)"), ACT.Gelu,
                                     bias=b1sel[:, col:col + 1], scale=1 / W1_SCALE).then_inc(s_gelu, 1)

            for p in range(PAIRS):
                gelu(p, 0, 0)
                gelu(p, 0, 1)
                gelu(p, 1, 0)
                if p >= 1:
                    square(PAIRS + p - 1)
                gelu(p, 1, 1)
            square(2 * PAIRS - 1)

        @block.gpsimd
        def _(pool):
            words = signs[:].rearrange("q p n -> q (p n)").bitcast(F32)
            zw = REGIONS // 4
            nc.gpsimd.memset(words[:, 0:zw], 0.0).then_inc(s_zero, 1)
            nc.gpsimd.memset(words[:, zw:4 * zw], 0.0).then_inc(s_zero, 1)
            nc.gpsimd.memset(words[:, 4 * zw:], 0.0).then_inc(s_zero, 1)

            def product(p):
                pool.wait_ge(s_edge, p + 1)
                nc.gpsimd.tensor_tensor(out=signs[:, p, PADDED + 1:2 * PADDED - 1], in0=edge[:, 1:PADDED - 1],
                                        in1=signs[:, p, 1:PADDED - 1], op=ALU.mult, saturate=False).then_inc(s_prod, 1)

            def token_low(p):
                pool.wait_ge(s_uh, p + 1)
                nc.gpsimd.tensor_tensor(out=ul[:, p % 2, :], in0=us[:, p, :], in1=uh[:, p % 2, :],
                                        op=ALU.subtract).then_inc(s_ul, 1)

            pool.wait_ge(s_zero, 3)
            for p in range(1, 3):
                product(p)
            for p in range(PAIRS):
                if p + 3 < PAIRS:
                    product(p + 3)
                if p >= 3:
                    token_low(p - 3)
            for p in range(PAIRS - 3, PAIRS):
                token_low(p)

            table = w2f[:].rearrange("q e d -> q (e d)")

            def select_w2(p):
                for k in range(2):
                    for b in range(2):
                        col = k * 16 + b * PAIRS + p
                        e = pool.value_load(offs[0:1, 1, col:col + 1], min_val=0, max_val=(EXPERTS - 1) * CH)
                        nc.gpsimd.tensor_tensor(out=w2sel[:, k, b, p, :], in0=table[:, bass.ds(e, CH)],
                                                in1=picks[:, 0, k, b * PAIRS + p:b * PAIRS + p + 1].broadcast_to([128, CH]),
                                                op=ALU.mult).then_inc(s_w2s, 1)

            pool.wait_ge(s_route["offsets"], 2)
            pool.wait_ge(s_route["picks"], 1)
            pool.wait_ge(s_w2c, 4)
            select_w2(0)
            for p in range(PAIRS):
                if p + 1 < PAIRS:
                    select_w2(p + 1)
                nc.gpsimd.tensor_tensor(out=xs[:, p, :], in0=xs[:, p, :], in1=conv16[:, p, :],
                                        op=ALU.add).then_inc(s_res, 1)

        @block.vector
        def _(dve):
            nc.vector.memset(rstd_s[:], 0.0).then_inc(s_zero_v, 1)
            nc.vector.memset(ublk[:], 0.0).then_inc(s_ublk, 1)

            def edges(p):
                dve.wait_ge(s_sign, p + 1)
                if p == 1:
                    dve.wait_ge(s_prod0, 1)
                elif p >= 2:
                    dve.wait_ge(s_prod, p - 1)
                nc.vector.tensor_tensor(out=edge[:, 1:PADDED - 1], in0=signs[:, p, 0:PADDED - 2],
                                        in1=signs[:, p, 2:PADDED], op=ALU.mult).then_inc(s_edge, 1)

            def order_conv_weights():
                dve.wait_ge(s_cw_sign, 1)
                nc.vector.tensor_tensor(out=cwp[:], in0=cws[:, :, 0, :], in1=cws[:, :, 1, :], op=ALU.mult).then_inc(s_cw_prep, 1)
                dve.wait_ge(s_cw_prep, 1)
                nc.vector.scalar_tensor_tensor(out=cwo[:, 0, :, 1, 0, :], in0=cwp[:], scalar=-0.5, in1=cws[:, :, 2, :],
                                               op0=ALU.mult, op1=ALU.mult).then_inc(s_cw_ord, 1)
                nc.vector.scalar_tensor_tensor(out=cwo[:, 1, :, 1, 1, :], in0=cwp[:], scalar=-0.5, in1=cws[:, :, 2, :],
                                               op0=ALU.mult, op1=ALU.mult).then_inc(s_cw_ord, 1)
                nc.vector.tensor_scalar(cwo[:, 0, :, 0, :, :], cws[:, :, 0:2, :], 0.5, None, ALU.mult).then_inc(s_cw_ord, 1)
                for t in range(2):
                    i = nc.vector.tensor_scalar(cwo[:, 1, :, 0, t, :], cws[:, :, 1 - t, :], 0.5, None, ALU.mult)
                    if t == 1:
                        i.then_inc(s_cw_ord, 1)
                nc.vector.tensor_scalar(cwo[:, 0, :, 1, 1, :], cws[:, :, 2, :], 0.5, None, ALU.mult).then_inc(s_cw_ord, 1)
                nc.vector.tensor_scalar(cwo[:, 1, :, 1, 0, :], cws[:, :, 2, :], 0.5, None, ALU.mult).then_inc(s_cw_ord, 1)

            def expert_weights():
                dve.wait_ge(s_w1h, 1)
                nc.vector.scalar_tensor_tensor(out=w1s[:, :, 1, :], in0=w1f[:], scalar=W1_SCALE, in1=w1s[:, :, 0, :],
                                               op0=ALU.mult, op1=ALU.subtract).then_inc(s_w1l, 1)
                dve.wait_ge(s_w, 16 * 10)
                nc.vector.tensor_reduce(w2m[:], w2f[:], AX.X, ALU.add).then_inc(s_w2c, 1)
                nc.vector.tensor_reduce(b2m[:], b2f[:], AX.X, ALU.add).then_inc(s_w2c, 1)
                dve.wait_ge(s_w2c, 2)
                mean = w2m[:].rearrange("q (e o) -> q e o", o=1).broadcast_to([128, EXPERTS, CH])
                nc.vector.scalar_tensor_tensor(out=w2f[:], in0=mean, scalar=-1.0 / CH, in1=w2f[:],
                                               op0=ALU.mult, op1=ALU.add).then_inc(s_w2c, 1)
                nc.vector.scalar_tensor_tensor(out=b2f[:], in0=b2m[:].broadcast_to([EXPERTS, CH]), scalar=-1.0 / CH,
                                               in1=b2f[:], op0=ALU.mult, op1=ALU.add).then_inc(s_w2c, 1)

            def inverse_deviations(g):
                pairs = WIDE if g < GROUPS else 1
                run, blocks = pairs * QUARTER, pairs * 8
                v, y, a, b = (stat[:, i, 0:blocks, :] for i in range(4))
                dve.wait_ge(s_var, g + 1)
                nc.vector.transpose(var_t[:, 0:run], var_ps[:, 0:run]).then_inc(s_vt, 1)
                dve.wait_ge(s_vt, g + 1)
                last = [NEWTON_STEPS * g]

                def step(i):
                    last[0] += 1
                    i.then_inc(s_newton, 1)
                    dve.wait_ge(s_newton, last[0])

                V = nc.vector
                step(V.tensor_scalar(v, var_t[:, 0:run].rearrange("q (a c) -> q a c", c=32)[:, :, 0:2],
                                     RSTD_SCALE ** -2, EPS_LN * RSTD_SCALE ** -2, ALU.mult, ALU.add))
                step(V.tensor_scalar(y.bitcast(I32), v.bitcast(I32), -0.5, MAGIC, ALU.mult, ALU.add))
                step(V.tensor_tensor(out=a, in0=y, in1=y, op=ALU.mult))
                step(V.tensor_tensor(out=a, in0=a, in1=v, op=ALU.mult))
                step(V.tensor_scalar(b, a, 0.375, -1.25, ALU.mult, ALU.add))
                step(V.tensor_tensor(out=b, in0=b, in1=a, op=ALU.mult))
                step(V.scalar_tensor_tensor(out=y, in0=b, scalar=1.875, in1=y, op0=ALU.add, op1=ALU.mult))
                step(V.tensor_tensor(out=a, in0=y, in1=y, op=ALU.mult))
                step(V.scalar_tensor_tensor(out=a, in0=a, scalar=-0.5, in1=v, op0=ALU.mult, op1=ALU.mult))
                step(V.scalar_tensor_tensor(out=y, in0=a, scalar=1.5, in1=y, op0=ALU.add, op1=ALU.mult))
                if g == 0:
                    dve.wait_ge(s_zero_v, 1)
                step(V.tensor_copy(rstd_s[:, 0:blocks, 0:2], y))
                step(V.tensor_tensor(out=rstd_s[:, 0:blocks, 2:4], in0=y, in1=rstd_s[:, 0:blocks, 0:2],
                                     op=ALU.subtract))
                assert last[0] == NEWTON_STEPS * (g + 1)
                if 1 <= g <= GROUPS:
                    dve.wait_ge(s_sp, WIDE * g)
                elif g > GROUPS:
                    dve.wait_ge(s_sp2, 2 * (g - GROUPS))
                nc.vector.transpose(rstd_t[:, 0:run], rstd_s[:, 0:blocks, :].rearrange("q a c -> q (a c)")).then_inc(s_rt, 1)

            def residual(p):
                for h in range(2):
                    half = us[:, p, h * HALF:(h + 1) * HALF]
                    dve.wait_ge(s_cc, 2 * p + h + 1)
                    nc.vector.tensor_tensor(out=half, in0=half, in1=conv_ps[:, h, :], op=ALU.add).then_inc(s_xc, 1)

            def tokens(p):
                dve.wait_ge(s_sp, p + 1)
                nc.vector.scalar_tensor_tensor(out=us[:, p, :], in0=us[:, p, :], scalar=1.0,
                                               in1=spread_ps[p].rearrange("q h n -> q (h n)"), op0=ALU.mult, op1=ALU.mult,
                                               accum_out=usum[:, p:p + 1]).then_inc(s_u, 1)

            order_conv_weights()
            edges(0)
            dve.wait_ge(s_edge, 1)
            nc.vector.tensor_tensor(out=signs[:, 0, PADDED + 1:2 * PADDED - 1], in0=edge[:, 1:PADDED - 1],
                                    in1=signs[:, 0, 1:PADDED - 1], op=ALU.mult, saturate=False).then_inc(s_prod0, 1)
            dve.wait_ge(s_cw_tr, 1)
            nc.vector.tensor_copy(cwT[:].rearrange("q b r t o -> q (b r t o)"),
                                  misc_ps[:, 0:384].bitcast(F16)).then_inc(s_cw_done, 1)
            for p in range(1, 3):
                edges(p)
            expert_weights()
            for p in range(PAIRS):
                residual(p)
                if p >= 3:
                    tokens(p - 3)
                if p >= WIDE and p % WIDE == 0:
                    inverse_deviations(p // WIDE - 1)
                if p + 3 < PAIRS:
                    edges(p + 3)
            tokens(PAIRS - 3)
            inverse_deviations(GROUPS - 1)
            tokens(PAIRS - 2)
            tokens(PAIRS - 1)

            dve.wait_ge(s_u, PAIRS)
            dve.wait_ge(s_ublk, 1)
            nc.vector.tensor_copy(ublk[LO, 0, :], usum[LO, :]).then_inc(s_ublk, 1)
            nc.vector.tensor_copy(ublk[HI, 1, :], usum[HI, :]).then_inc(s_ublk, 1)
            V = nc.vector

            def then(name, i, value=1):
                i.then_inc(s_route[name], 1)
                dve.wait_ge(s_route[name], value)

            dve.wait_ge(s_route_pe, 1)
            then("logits", V.scalar_tensor_tensor(out=logit[:, 0, :], in0=misc_ps[0:16, 0:8], scalar=1.0 / TOK,
                                                  in1=brs[:], op0=ALU.mult, op1=ALU.add))
            V.tensor_reduce(neg_top[:, 0:1], logit[:, 0, :], AX.X, ALU.max, negate=True).then_inc(s_route["shift1"], 1)
            dve.wait_ge(s_route_act, 1)
            then("inverse", V.reciprocal(inverse[:, 0:1], total[:, 0:1]), 1)
            V.tensor_scalar(weight[:, 0, :], expo[:, 0, :], inverse[:, 0:1], None,
                            ALU.mult).then_inc(s_route["weights1"], 1)
            dve.wait_ge(s_route_pe, 2)
            then("relief", V.reciprocal(relief[:], misc_ps[0:16, 8:16]))
            then("scaled", V.scalar_tensor_tensor(out=logit[:, 1, :], in0=relief[:], scalar=1.0, in1=weight[:, 0, :],
                                                  op0=ALU.min, op1=ALU.mult))
            V.tensor_reduce(neg_top[:, 1:2], logit[:, 1, :], AX.X, ALU.max, negate=True).then_inc(s_route["shift2"], 1)
            dve.wait_ge(s_route_act, 2)
            then("inverse", V.reciprocal(inverse[:, 1:2], total[:, 1:2]), 2)
            then("weights2", V.tensor_scalar(weight[:, 1, :], expo[:, 1, :], inverse[:, 1:2], None, ALU.mult))
            V.tensor_reduce(neg_top[:, 2:3], weight[:, 1, :], AX.X, ALU.max, negate=True).then_inc(s_route["negated"], 1)
            then("top", V.max(top8[:], weight[:, 1, :]))
            then("top", V.max_index(top8_at[:], top8[:], weight[:, 1, :]), 2)
            eye = c32[0:16, C_EYE:C_EYE + 16].rearrange("q (o n) -> q o n", o=1).broadcast_to([16, 2, 16])
            V.tensor_tensor(out=diag[:, 1, :, :], in0=eye,
                            in1=top8_at[:, 0:2].rearrange("q (k o) -> q k o", o=1).broadcast_to([16, 2, 16]),
                            op=ALU.mult).then_inc(s_route["diagonals"], 1)
            dve.wait_ge(s_route_act, 3)
            then("inverse", V.reciprocal(inverse[:, 2:3], total[:, 2:3]), 3)
            V.scalar_tensor_tensor(out=diag[:, 0, :, :], in0=eye, scalar=inverse[:, 2:3],
                                   in1=top_exp[:].rearrange("q (k o) -> q k o", o=1).broadcast_to([16, 2, 16]),
                                   op0=ALU.mult, op1=ALU.mult).then_inc(s_route["diagonals"], 1)
            dve.wait_ge(s_route_pe, 3)
            pk = misc_ps[0:1, 48:80]
            V.tensor_scalar(offs[0:1, 0, :], pk, float(2 * FFN), None, ALU.mult).then_inc(s_route["offsets"], 1)
            V.tensor_scalar(hot[:], misc_ps[0:8, 48:80], c32[0:8, C_PART:C_PART + 1], None,
                            ALU.is_equal).then_inc(s_route["hot"], 1)
            V.tensor_scalar(offs[0:1, 1, :], pk, float(CH), None, ALU.mult).then_inc(s_route["offsets"], 1)
            then("picks", V.tensor_copy(picks[:].rearrange("q a k n -> q (a k n)"), misc_ps[:, 16:80]))
            dve.wait_ge(s_route_pe, 4)
            V.tensor_copy(b1sel[:], b1_ps).then_inc(s_route["biases"], 1)
            dve.wait_ge(s_route["hot"], 1)
            then("dense", V.tensor_tensor(out=wden[:].rearrange("q k n -> q (k n)"), in0=hot[:],
                                          in1=picks[0:8, 0, :, :].rearrange("q k n -> q (k n)"), op=ALU.mult))
            then("dense", V.tensor_tensor(out=wden[:, 0, :], in0=wden[:, 0, :], in1=wden[:, 1, :], op=ALU.add), 2)
            dve.wait_ge(s_route_pe, 5)
            then("biases", V.tensor_copy(b2sel[:], b2_ps), 2)

            def mixture(p):
                dve.wait_ge(s_down, 2 * p + 2)
                nc.vector.scalar_tensor_tensor(out=us[:, p, :], in0=y_ps.rearrange("q h n -> q (h n)"),
                                               scalar=b2sel[:, p:p + 1], in1=us[:, p, :],
                                               op0=ALU.add, op1=ALU.add).then_inc(s_z, 1)

            def normalise(p, h):
                dve.wait_ge(s_sp2, 2 * p + h + 1)
                half = us[:, p, h * HALF:(h + 1) * HALF]
                nc.vector.scalar_tensor_tensor(out=half, in0=half, scalar=gam[:], in1=spread2_ps,
                                               op0=ALU.mult, op1=ALU.mult).then_inc(s_zr, 1)

            def output(p):
                dve.wait_ge(s_zr, 2 * p + 2)
                dve.wait_ge(s_res, p + 1)
                nc.vector.scalar_tensor_tensor(out=xs[:, p, :], in0=us[:, p, :], scalar=bet[:], in1=xs[:, p, :],
                                               op0=ALU.add, op1=ALU.add).then_inc(s_o, 1)

            for p in range(PAIRS):
                if p >= 1:
                    mixture(p - 1)
                if p >= 2:
                    normalise(p - 2, 0)
                    normalise(p - 2, 1)
                    output(p - 2)
                if p >= 1:
                    inverse_deviations(GROUPS + p - 1)
            mixture(PAIRS - 1)
            normalise(PAIRS - 2, 0)
            normalise(PAIRS - 2, 1)
            inverse_deviations(GROUPS + PAIRS - 1)
            output(PAIRS - 2)
            normalise(PAIRS - 1, 0)
            normalise(PAIRS - 1, 1)
            output(PAIRS - 1)


_INS = ["x", "L0_conv_weight", "L0_ffn_Wr", "L0_ffn_br", "L0_ffn_W1", "L0_ffn_b1", "L0_ffn_W2", "L0_ffn_b2",
        "L0_ffn_gamma", "L0_ffn_beta"]


def kernel(**inputs):
    import concourse.bacc as _bacc
    from concourse import mybir as _mybir
    from concourse.bass_utils import run_bass_kernel_spmd as _run

    nc = _bacc.Bacc("TRN2", target_bir_lowering=False, num_devices=1)
    arrays, args = {}, []
    c32, c16 = constants()
    for name, a in [(n, np.ascontiguousarray(inputs[n])) for n in _INS] + [("const32", c32), ("const16", c16)]:
        arrays[f"in_{name}"] = a
        args.append(nc.dram_tensor(f"in_{name}", a.shape, _mybir.dt.from_np(a.dtype), kind="ExternalInput").ap())
    args.append(nc.dram_tensor("out_0", (N_IMG, CH, H, W), _mybir.dt.float32, kind="ExternalOutput").ap())
    metaformer(nc, *args)
    return _run(nc, [arrays], core_ids=[0]).results[0]["out_0"]
```

```python
from contextlib import ExitStack

import numpy as np

import concourse.bass as bass
from concourse import mybir

N_IMG, CH, H, W = 16, 64, 32, 32
TOK = H * W
PAIRS = N_IMG // 2
EXPERTS, FFN = 8, 128
HALF = TOK // 2
ROWS_HALF = H // 2
PW = W + 2
PADDED = (H + 2) * PW
REGIONS = 2 * PADDED
QUARTER = TOK // 4
EPS_LN = 1e-5
CAPACITY = float(-(-N_IMG * TOK * 5 // (4 * EXPERTS)))
RSTD_SCALE = 128.0
W1_SCALE = 64.0

C_CENTER, C_SUM, C_IOTA8, C_PART, C_EYE, C_ONES = 0, 128, 160, 168, 169, 185
C_LOAD = C_ONES + 128
C32 = C_LOAD + 16
C_NEGMEAN, C_SPREAD, C_ID16 = 0, 128, 640
C16 = C_ID16 + 64


GROUP = [(0, 1), (2, 3), (4, 5), (6, 7)]
GROUPS = len(GROUP)
GROUP += [(PAIRS + p,) for p in range(PAIRS)]
GROUP_OF = {n: g for g, members in enumerate(GROUP) for n in members}
SQ_SLOTS = 3
SQ_HALVES = (PAIRS - 1, 2 * PAIRS - 1)
SPREAD_BANK = (5, 5, 5, 0, 5, 2, 5, 2)
EARLY = 4
ASIDE = 3
DVE_EDGES = 3
FILL_START, FILL_CONV, FILL_SPREAD, FILL_ROUTE, FILL_LAST = 7, 4, (17, 3), (8, 3, 6, 1), (6, 12)
MAGIC = float(0x5F3759DF)
ZERO_OF = [0, 1, 1, 1, 2, 2, 2, 2]


def tokens_ready(p):
    return p + 1 - (p > ASIDE)


def squares_done(n, h):
    return n + 1 + sum(m < n for m in SQ_HALVES) + (n in SQ_HALVES and h == 1)


def constants():
    c = np.zeros((128, C32), np.float32)
    for b in (0, 64):
        c[b:b + 64, C_CENTER + b:C_CENTER + b + 64] = np.eye(64) - 1.0 / CH
        c[b:b + 64, C_SUM + b // 64] = 1.0 / CH
    c[:, C_IOTA8:C_IOTA8 + 8] = np.arange(8) - 8
    c[:, C_PART] = np.arange(128)
    c[0:16, C_EYE:C_EYE + 16] = np.eye(16)
    c[:, C_ONES:C_ONES + 128] = 1.0
    c[:, C_LOAD:C_LOAD + 16] = TOK / CAPACITY
    d = np.zeros((128, C16), np.float16)
    for b in (0, 64):
        d[b:b + 64, C_NEGMEAN + b:C_NEGMEAN + b + 64] = -1.0 / CH
    for j in range(4):
        for b in (0, 1):
            for part in (0, 2):
                d[32 * j + part + b, C_SPREAD + 128 * j + 64 * b:C_SPREAD + 128 * j + 64 * b + 64] = 1 / RSTD_SCALE
    d[0:64, C_ID16:C_ID16 + 64] = np.eye(64)
    return c, d


def metaformer(nc, x, conv_w, Wr, br, W1, b1, W2, b2, gamma, beta, const32, const16, out):
    F32, F16, I32, F8 = mybir.dt.float32, mybir.dt.float16, mybir.dt.int32, mybir.dt.float8e4
    ALU, ACT, AX = mybir.AluOpType, mybir.ActivationFunctionType, mybir.AxisListType
    LO, HI = slice(0, 64), slice(64, 128)
    IMG = (LO, HI)

    x_pairs = x.rearrange("(q b) c h w -> q (b c) (h w)", b=2)
    out_pairs = out.rearrange("(q b) c h w -> q (b c) (h w)", b=2)

    with ExitStack() as ctx:
        def sb(name, shape, dt=F32):
            return ctx.enter_context(nc.sbuf_tensor(name, shape, dt))

        def sem(name):
            return ctx.enter_context(nc.semaphore(name))

        xs = sb("xs", [128, PAIRS, TOK])
        us = sb("us", [128, PAIRS, TOK])
        conv16 = sb("conv16", [128, PAIRS, TOK], F16)
        split = sb("split", [128, PAIRS, 2, TOK], F16)
        signs = sb("signs", [128, PAIRS, REGIONS], F8)
        stack = sb("stack", [128, 3, 2, REGIONS], F8)
        zeros = sb("zeros", [128, HALF], F16)
        edge = sb("edge", [128, 2, H, W], F16)
        uh = sb("uh", [128, 2, TOK], F16)
        ul = sb("ul", [128, 2, TOK], F16)
        dev = edge[:].rearrange("q s r c -> q (s r c)").bitcast(F32)
        sq = sb("sq", [128, SQ_SLOTS, TOK])
        hid = signs[:].rearrange("q p n -> q (p n)").bitcast(F32)[:, 0:4 * TOK]\
            .rearrange("q (k b n) -> q k b n", k=2, b=2)
        var_t = sb("var_t", [128, HALF])
        stat = sb("stat", [128, 4, 16, 2])
        rstd_s = sb("rstd_s", [128, 16, 32], F16)
        rstd_t = sb("rstd_t", [128, 2, HALF], F16)
        c32 = sb("c32", [128, C32])
        c16 = sb("c16", [128, C16], F16)
        cw = sb("cw", [64, 3, 3, 64])
        cws = sb("cws", [64, 3, 3, 64], F16)
        cwp = sb("cwp", [64, 3, 64], F16)
        cwo = sb("cwo", [64, 2, 3, 2, 2, 64], F16)
        cwT = sb("cwT", [128, 2, 3, 2, 64], F16)
        w1f = sb("w1f", [128, EXPERTS, FFN])
        w1s = sb("w1s", [128, EXPERTS, 2, FFN], F16)
        w2f = sb("w2f", [128, EXPERTS, CH])
        w2m = sb("w2m", [128, EXPERTS])
        w2sel = sb("w2sel", [128, 2, 2, PAIRS, CH])
        b1f = sb("b1f", [EXPERTS, FFN])
        b2f = sb("b2f", [EXPERTS, CH])
        b2m = sb("b2m", [EXPERTS, 1])
        wr = sb("wr", [128, EXPERTS])
        brs = sb("brs", [N_IMG, EXPERTS])
        gam = sb("gam", [128, 1])
        bet = sb("bet", [128, 1])
        warm = sb("warm", [128, 1])
        usum = sb("usum", [128, PAIRS])
        ublk = sb("ublk", [128, 2, PAIRS])
        logit, expo, weight = (sb(n, [N_IMG, 2, EXPERTS]) for n in ("logit", "expo", "weight"))
        relief = sb("relief", [N_IMG, EXPERTS])
        neg_top = sb("neg_top", [N_IMG, 2])
        total = sb("total", [N_IMG, 3])
        inverse = sb("inverse", [N_IMG, 3])
        top8 = sb("top8", [N_IMG, 8])
        top8_at = sb("top8_at", [N_IMG, 8], mybir.dt.uint32)
        top_shifted = sb("top_shifted", [N_IMG, 2])
        top_exp = sb("top_exp", [N_IMG, 2])
        diag = sb("diag", [N_IMG, 2, 2, N_IMG])
        picks = sb("picks", [128, 2, N_IMG])
        offs = sb("offs", [1, 2, 32], I32)
        hot = sb("hot", [EXPERTS, 32])
        wden = sb("wden", [EXPERTS, 2, N_IMG])
        b1sel = sb("b1sel", [128, 32])
        b2sel = sb("b2sel", [128, PAIRS])

        ps = ctx.enter_context(nc.psum_tensor("ps", [128, 8, 512], F32))
        cen_ps = [(ps[:, b, :], ps[:, c, :]) for b, c in ((0, 1), (5, 6), (0, 1), (4, 7)) + ((0, 1),) * (PAIRS - 4)]
        conv_ps = [ps[:, b:b + 2, :] for b in (2,) * (PAIRS - 1) + (0,)]
        var_ps = ps[:, 4, :]
        spread_ps = [ps[:, b:b + 2, :] for b in SPREAD_BANK]
        early_ps = ps[:, 7, :]
        picks_ps = (ps[:, 5, 0:32], ps[:, 6, 0:32])
        b1_ps = ps[:, 4, 0:32]
        b2_ps = ps[:, 7, 112:112 + PAIRS]
        hid_ps = (ps[:, 0:2, :], ps[:, 2:4, :])
        y_ps = ps[:, 5:7, :]

        def out_spread_ps(p, h):
            return ps[:, 4 + 3 * (1 - h), :] if p < PAIRS - 2 else ps[:, 2 * (PAIRS - 1 - p) + h, :]


        s_x0 = [sem(f"x_half_loaded{h}") for h in range(2)]
        s_x = [sem(f"x_loaded{p}") for p in range(PAIRS)]
        s_c32 = sem("const32_loaded")
        s_c16c = sem("const16_loaded")
        s_cw = sem("conv_weights_loaded")
        s_w1 = sem("w1_loaded")
        s_w2 = sem("w2_loaded")
        s_w = sem("weights_loaded")
        s_zero = sem("zeroed")
        s_zero_v = sem("rstd_columns_zeroed")
        s_cw_sign = sem("conv_weight_signs")
        s_cw_prep = sem("conv_weight_steps")
        s_cw_ord = sem("conv_weights_ordered")
        s_cw_tr = sem("conv_weights_turned")
        s_cw_done = sem("conv_weights_ready")
        s_w1h = sem("w1_high")
        s_w1l = sem("w1_low")
        s_w2c = sem("w2_steps")
        s_cen = sem("centred")
        s_sign0 = sem("first_signs_done")
        s_sign = sem("signs_done")
        s_keep = sem("centred_kept")
        s_edge = sem("edge_products")
        s_prod0 = sem("first_products_done")
        s_prod = sem("products_done")
        s_stack = [sem(f"stacked{b}") for b in range(3)]
        s_conv = sem("conv_done")
        s_c16 = sem("conv16_done")
        s_cc = sem("conv_centred")
        s_xc = sem("residual_centred")
        s_sq = sem("squares_done")
        s_var = sem("variances_done")
        s_vt = sem("variances_turned")
        s_newton = sem("rstd_steps")
        s_high = sem("rstd_high_part")
        s_rt = sem("rstd_rows")
        s_sp = sem("rstd_spread")
        s_u = sem("tokens_done")
        s_uh = sem("token_high")
        s_ul = sem("token_low")
        s_split = [sem(f"token_split{p}") for p in range(PAIRS)]
        s_ublk = sem("token_sums")
        s_route_pe = sem("route_products")
        s_route = {n: sem(n) for n in (
            "logits", "shift1", "weights1", "relief", "scaled", "shift2", "shift3", "top", "inverse",
            "diagonals", "offsets", "picks", "hot", "dense", "biases")}
        s_route_act = sem("route_scalar_steps")
        s_res = sem("residual_done")
        s_w2s = sem("w2_selected")
        s_up = sem("up_projected")
        s_gelu = sem("hidden_done")
        s_down = sem("down_projected")
        s_z = sem("mixture_centred")
        s_zr = sem("normalised")
        s_sp2 = sem("rstd_spread2")
        s_o = sem("output_done")
        s_dev = sem("deviation_kept")
        s_u_pool = sem("tokens_done_by_pool")
        s_usum = sem("tokens_summed")
        s_gr = sem("gamma_over_deviation")
        s_zr_pool = sem("normalised_by_pool")
        s_beta = sem("beta_added")
        s_o_pool = sem("output_done_by_pool")
        s_out = sem("output_stored")

        block = ctx.enter_context(nc.Block())

        def padded(ap):
            return ap.rearrange("q (r c) -> q r c", c=PW)

        def rows_of(p, region, h=None, shift=0):
            r0, r1 = (0, H) if h is None else (h * ROWS_HALF, (h + 1) * ROWS_HALF)
            grid = padded(signs[:, p, region * PADDED:(region + 1) * PADDED])
            return grid[:, 1 + r0:1 + r1, 1 + shift:1 + shift + W], edge[:, p % 2, r0:r1, :]

        def edge_product(engine, p, h=None):
            left, products = rows_of(p, 0, h, -1)
            right, _ = rows_of(p, 0, h, 1)
            return engine.tensor_tensor(out=products, in0=left, in1=right, op=ALU.mult)

        def sign_product(engine, p, h=None):
            middle, edges = rows_of(p, 0, h)
            products, _ = rows_of(p, 1, h)
            return engine.tensor_tensor(out=products, in0=edges, in1=middle, op=ALU.mult, saturate=False)

        @block.sync
        def _(sp):
            for h in range(2):
                at = slice(h * HALF, (h + 1) * HALF)
                sp.dma_start(xs[:, 0, at], x_pairs[0][:, at]).then_inc(s_x0[h], 16)
            for p in range(1, 4):
                sp.dma_start(xs[:, p, :], x_pairs[p]).then_inc(s_x[p], 16)

            def load_weights(p):
                if p == 1:
                    for b in range(2):
                        sp.dma_start(w1f[IMG[b], :, :], W1.rearrange("e d f -> d e f")).then_inc(s_w1, 16)
                elif p == 2:
                    sp.dma_start(w2f[:], W2.rearrange("e f d -> f e d")).then_inc(s_w2, 16)
                    sp.dma_start(b2f[:], b2).then_inc(s_w2, 16)
                elif p == 3:
                    sp.dma_start(b1f[:], b1).then_inc(s_w, 16)
                    sp.dma_start(brs[:], br.rearrange("(o e) -> o e", o=1).broadcast_to([N_IMG, EXPERTS]))\
                        .then_inc(s_w, 16)
                elif p in (4, 5):
                    b = IMG[p - 4]
                    sp.dma_start(wr[b, :], Wr).then_inc(s_w, 16)
                    sp.dma_start(gam[b, :], gamma.rearrange("(d o) -> d o", o=1)).then_inc(s_w, 16)
                    sp.dma_start(bet[b, :], beta.rearrange("(d o) -> d o", o=1)).then_inc(s_w, 16)

            def stack_signs(p, b):
                shifted = signs[IMG[b], p, 1:PADDED].rearrange("q (o n) -> q o n", o=1)\
                    .broadcast_to([64, 2, PADDED - 1])
                dst = stack[IMG[1 - b], p % 3, b, :].rearrange("q (o n) -> q o n", o=2)[:, :, 0:PADDED - 1]
                sp.dma_start(dst, shifted).then_inc(s_stack[p % 3], 16)

            def stack_own(p, b, regions):
                at = slice(PADDED * regions[0], PADDED * (regions[-1] + 1))
                sp.dma_start(stack[IMG[b], p % 3, b, at], signs[IMG[b], p, at]).then_inc(s_stack[p % 3], 16)

            def stack_pair(p):
                if p == 0:
                    sp.wait_ge(s_sign0, 2)
                    for b in range(2):
                        stack_signs(0, b)
                        stack_own(0, b, (0,))
                    sp.wait_ge(s_prod0, 2)
                    for b in range(2):
                        stack_own(0, b, (1,))
                    return
                sp.wait_ge(s_prod, p)
                if p >= 3:
                    sp.wait_ge(s_conv, 2 * (p - 2))
                for b in range(2):
                    stack_own(p, b, (0, 1))
                    stack_signs(p, b)

            def split_pair(p):
                sp.wait_ge(s_ul, p + 1)
                for b in range(2):
                    sp.dma_start(split[IMG[b], p, b, :], uh[IMG[b], p % 2, :]).then_inc(s_split[p], 16)
                    sp.dma_start(split[IMG[1 - b], p, b, :], ul[IMG[b], p % 2, :]).then_inc(s_split[p], 16)

            for p in range(PAIRS):
                stack_pair(p)
                if p + 4 < PAIRS:
                    sp.dma_start(xs[:, p + 4, :], x_pairs[p + 4]).then_inc(s_x[p + 4], 16)
                load_weights(p)
            for p in range(EARLY):
                split_pair(p)
            for p in range(PAIRS - 2):
                if p + EARLY < PAIRS:
                    split_pair(p + EARLY)
                if p < PAIRS - 3:
                    sp.wait_ge(s_o, p + 1)
                else:
                    sp.wait_ge(s_o_pool, 1)
                sp.dma_start(out_pairs[p], xs[:, p, :]).then_inc(s_out, 16)
            for p, h in ((PAIRS - 2, 1), (PAIRS - 2, 0), (PAIRS - 1, 1), (PAIRS - 1, 0)):
                at = slice(h * HALF, (h + 1) * HALF)
                if p == PAIRS - 2:
                    sp.wait_ge(s_o_pool, 3 - h)
                elif h == 1:
                    sp.wait_ge(s_o, PAIRS - 3 + 1)
                else:
                    sp.wait_ge(s_o_pool, 4)
                sp.dma_start(out_pairs[p][:, at], xs[:, p, at]).then_inc(s_out, 16)
            sp.wait_ge(s_out, 16 * (PAIRS + 2))

        @block.tensor
        def _(pe):
            def centre(p, h):
                if p == 0:
                    pe.wait_ge(s_x0[h], 16)
                elif h == 0:
                    pe.wait_ge(s_x[p], 16)
                if p == 0 and h == 0:
                    pe.wait_ge(s_c32, 16)
                if p == 3 and h == 1:
                    pe.wait_ge(s_cw_done, 1)
                elif h == 0 and p in (2, 4):
                    pe.wait_ge(s_keep, p - 1)
                elif h == 0 and p > 4:
                    pe.wait_ge(s_keep, p)
                nc.tensor.matmul(cen_ps[p][h], c32[:, C_CENTER:C_CENTER + 128],
                                 xs[:, p, h * HALF:(h + 1) * HALF], start=True, stop=True).then_inc(s_cen, 1)

            def turn_conv_weights():
                pe.wait_ge(s_cw_ord, 7)
                pe.wait_ge(s_c16c, 16)
                tr = early_ps[:, 0:384].bitcast(F16).rearrange("q (n o) -> q n o", o=64)
                n = 0
                for b in range(2):
                    for r in range(3):
                        for h in range(2):
                            mm = nc.tensor.transpose(tr[:, n, :], cwo[:, b, r, h, :, :].rearrange("o t i -> o (t i)"),
                                                     c16[0:64, C_ID16:C_ID16 + 64])
                            n += 1
                mm.then_inc(s_cw_tr, 1)

            def convolve(p, halves=(0, 1)):
                if 0 in halves:
                    pe.wait_ge(s_stack[p % 3], 64 * (p // 3 + 1) + (32 if p % 3 == 0 else 0))
                if p == 0:
                    pe.wait_ge(s_cw_done, 1)
                for h in halves:
                    if 1 <= p < PAIRS - 1:
                        pe.wait_ge(s_xc, 2 * (p - 1) + h + 1)
                    elif p == PAIRS - 1:
                        pe.wait_ge(s_dev, 1)
                    for r in range(3):
                        for t in range(2):
                            for b in range(2):
                                rows = padded(stack[:, p % 3, b, t * PADDED:(t + 1) * PADDED])
                                at = ROWS_HALF * h + r
                                mm = nc.tensor.matmul(conv_ps[p][IMG[b], h, :], cwT[:, b, r, t, :],
                                                      rows[:, at:at + ROWS_HALF, t:t + W],
                                                      start=(r == 0 and t == 0), stop=(r == 2 and t == 1),
                                                      skip_group_check=True)
                    mm.then_inc(s_conv, 1)

            def centre_conv(p, h):
                pe.wait_ge(s_c16, 2 * p + h + 1)
                nc.tensor.matmul(conv_ps[p][:, h, :], c16[:, C_NEGMEAN:C_NEGMEAN + 128],
                                 conv16[:, p, h * HALF:(h + 1) * HALF], start=False, stop=True,
                                 skip_group_check=True).then_inc(s_cc, 1)

            def variances(g):
                pairs = len(GROUP[g])
                if g == 0:
                    pe.wait_ge(s_keep, 4)
                else:
                    pe.wait_ge(s_vt, g)
                if GROUPS < g < GROUPS + PAIRS - 1:
                    pe.wait_ge(s_zr, 2 * (g - GROUPS))
                run = pairs * QUARTER
                for j in range(4):
                    n, at = GROUP[g][j * run // TOK], j * run % TOK
                    pe.wait_ge(s_sq, squares_done(n, at // HALF))
                    runs = sq[:, n % SQ_SLOTS, at:at + run]
                    mm = nc.tensor.matmul(var_ps[32 * j:32 * j + 32, 0:run], c32[:, C_SUM:C_SUM + 32],
                                          runs, start=True, stop=True)
                mm.then_inc(s_var, 1)

            def spread(p):
                g = GROUP_OF[p]
                if p == GROUP[g][0]:
                    pe.wait_ge(s_rt, g + 1)
                if p == 0:
                    pe.wait_ge(s_keep, 2)
                elif p == 3:
                    pe.wait_ge(s_keep, PAIRS)
                elif p == 5:
                    pe.wait_ge(s_xc, 2 * (PAIRS - 1))
                else:
                    before = max(q for q in range(p) if SPREAD_BANK[q] == SPREAD_BANK[p])
                    pe.wait_ge(s_u, tokens_ready(before))
                for h in range(2):
                    if len(GROUP[g]) == 1:
                        for j in range(2):
                            q = 2 * h + j
                            mm = nc.tensor.matmul(spread_ps[p][:, h, j * QUARTER:(j + 1) * QUARTER],
                                                  c16[:, C_SPREAD + 128 * q:C_SPREAD + 128 * (q + 1)],
                                                  rstd_t[:, g % 2, 0:QUARTER], start=True, stop=True)
                    else:
                        q = 2 * (p - GROUP[g][0]) + h
                        mm = nc.tensor.matmul(spread_ps[p][:, h, :],
                                              c16[:, C_SPREAD + 128 * q:C_SPREAD + 128 * (q + 1)],
                                              rstd_t[:, g % 2, :], start=True, stop=True)
                mm.then_inc(s_sp, 1)

            def fill(n, bank=4):
                for i in range(n):
                    nc.tensor.matmul(ps[:, bank, :], zeros[:, 0:128], zeros[:], start=True, stop=True)

            pe.wait_ge(s_zero_v, 1)
            fill(FILL_START)
            for p in range(4):
                for h in range(2):
                    centre(p, h)
                if p == 0:
                    turn_conv_weights()
            fill(FILL_CONV, 2)
            for p in range(4):
                convolve(p)
                centre(p + 4, 0)
                centre_conv(p, 0)
                centre_conv(p, 1)
                centre(p + 4, 1)
                if p == 2:
                    variances(0)
                elif p == 3:
                    spread(0)
            convolve(4, (0,))
            spread(1)
            convolve(4, (1,))
            centre_conv(4, 0)
            variances(1)
            centre_conv(4, 1)
            convolve(5)
            centre_conv(5, 0)
            centre_conv(5, 1)
            convolve(6, (0,))
            variances(2)
            spread(2)
            spread(3)
            convolve(6, (1,))
            centre_conv(6, 0)
            convolve(7, (0,))
            centre_conv(6, 1)
            convolve(7, (1,))
            centre_conv(7, 0)
            centre_conv(7, 1)
            spread(4)
            spread(5)
            variances(3)
            fill(FILL_SPREAD[0], 0)
            spread(6)
            fill(FILL_SPREAD[1], 0)
            spread(7)
            fill(FILL_ROUTE[0], 0)

            pe.wait_ge(s_ublk, 3)
            pe.wait_ge(s_w, 16 * 8)
            nc.tensor.matmul(early_ps[0:N_IMG, 0:8], ublk[:].rearrange("q b n -> q (b n)"), wr[:],
                             start=True, stop=True).then_inc(s_route_pe, 1)
            fill(FILL_ROUTE[1], 0)
            pe.wait_ge(s_route["weights1"], 1)
            nc.tensor.matmul(early_ps[0:N_IMG, 8:16], c32[0:N_IMG, C_LOAD:C_LOAD + N_IMG], weight[:, 0, :],
                             start=True, stop=True).then_inc(s_route_pe, 1)
            fill(FILL_ROUTE[2], 0)

            def picks_everywhere(i):
                pe.wait_ge(s_route["diagonals"], 2 - i)
                nc.tensor.matmul(picks_ps[i], c32[0:N_IMG, C_ONES:C_ONES + 128],
                                 diag[:, i, :, :].rearrange("q k n -> q (k n)"), start=True,
                                 stop=True).then_inc(s_route_pe, 1)

            picks_everywhere(1)
            fill(FILL_ROUTE[3], 0)

            def chosen_b1():
                pe.wait_ge(s_route["hot"], 1)
                nc.tensor.matmul(b1_ps, b1f[:], hot[:], start=True, stop=True).then_inc(s_route_pe, 1)

            def chosen_b2():
                pe.wait_ge(s_route["dense"], 2)
                for b in range(2):
                    mm = nc.tensor.matmul(b2_ps[IMG[b], :], b2f[:], wden[:, 0, b * PAIRS:(b + 1) * PAIRS],
                                          start=True, stop=True)
                mm.then_inc(s_route_pe, 1)

            def up(p, k, b):
                u = 2 * (2 * p + k) + b
                e = pe.value_load(offs[0:1, 0, k * 16 + b * PAIRS + p:k * 16 + b * PAIRS + p + 1],
                                  min_val=0, max_val=(EXPERTS - 1) * 2 * FFN)
                if u == 0:
                    chosen_b1()
                if k == 0:
                    pe.wait_ge(s_split[p], 64)
                if u >= 2:
                    pe.wait_ge(s_gelu, u - 1)
                table = w1s[:].rearrange("q e s f -> q (e s f)")
                for h in range(2):
                    for part in range(2):
                        mm = nc.tensor.matmul(hid_ps[b][:, h, :], table[:, bass.ds(e + part * FFN, FFN)],
                                              split[:, p, b, h * HALF:(h + 1) * HALF],
                                              start=(part == 0), stop=(part == 1))
                mm.then_inc(s_up, 1)

            def down(p, k, halves=(0, 1)):
                if 0 in halves:
                    pe.wait_ge(s_gelu, 2 * (2 * p + k) + 2)
                    pe.wait_ge(s_w2s, 4 * p + 2 * k + 2)
                    if k == 0 and p >= 1:
                        pe.wait_ge(s_z, p)
                for h in halves:
                    for b in range(2):
                        mm = nc.tensor.matmul(y_ps[IMG[b], h, :], w2sel[:, k, b, p, :],
                                              hid[:, k, b, h * HALF:(h + 1) * HALF],
                                              start=(k == 0), stop=(k == 1), skip_group_check=True)
                    mm.then_inc(s_down, 1)

            def spread_out(p, h):
                if h == 0:
                    pe.wait_ge(s_rt, GROUPS + p + 1)
                if p == 0 and h == 0:
                    pe.wait_ge(s_route["biases"], 2)
                if h == 0 and 1 <= p < PAIRS - 2:
                    pe.wait_ge(s_zr, 2 * p - 1)
                to = out_spread_ps(p, h)
                for j in range(2):
                    q = 2 * h + j
                    mm = nc.tensor.matmul(to[:, j * QUARTER:(j + 1) * QUARTER],
                                          c16[:, C_SPREAD + 128 * q:C_SPREAD + 128 * (q + 1)],
                                          rstd_t[:, (GROUPS + p) % 2, 0:QUARTER],
                                          start=True, stop=True)
                mm.then_inc(s_sp2, 1)

            pe.wait_ge(s_w1l, 1)
            pe.wait_ge(s_route["offsets"], 1)
            last = PAIRS - 1
            for p in range(PAIRS):
                up(p, 0, 0)
                if p == 0:
                    picks_everywhere(0)
                up(p, 0, 1)
                if p == 0:
                    chosen_b2()
                if p >= 1:
                    down(p - 1, 1)
                up(p, 1, 0)
                if p >= 2:
                    spread_out(p - 2, 0)
                up(p, 1, 1)
                if p >= 2:
                    spread_out(p - 2, 1)
                if p < last:
                    down(p, 0)
                if 1 <= p < last:
                    variances(GROUPS + p - 1)
            down(last, 0, (0,))
            variances(GROUPS + last - 1)
            down(last, 0, (1,))
            down(last, 1)
            fill(FILL_LAST[0], 0)
            variances(GROUPS + last)
            for h in range(2):
                spread_out(last - 1, h)
            fill(FILL_LAST[1], 0)
            for h in range(2):
                spread_out(last, h)

        @block.scalar
        def _(act):
            act.dma_start(c32[:], const32).then_inc(s_c32, 16)
            act.dma_start(cw[:], conv_w).then_inc(s_cw, 16)
            act.dma_start(c16[:], const16).then_inc(s_c16c, 16)
            act.wait_ge(s_cw, 16)
            nc.scalar.activation(cws[:], cw[:], ACT.Sign).then_inc(s_cw_sign, 1)

            def centred_parts(p):
                if p != 3:
                    at = (0, 1) if p != 1 else (5, 6)
                    return [(slice(0, H), slice(0, TOK), ps[:, at[0]:at[1] + 1, :].rearrange("q h n -> q (h n)"))]
                return [(slice(h * ROWS_HALF, (h + 1) * ROWS_HALF), slice(h * HALF, (h + 1) * HALF), cen_ps[p][h])
                        for h in range(2)]

            def signs_of(p):
                act.wait_ge(s_zero, 1 + ZERO_OF[p])
                grid = padded(signs[:, p, 0:PADDED])[:, 1:1 + H, 1:1 + W]
                if p == 0:
                    for h in range(2):
                        act.wait_ge(s_cen, h + 1)
                        nc.scalar.activation(grid[:, h * ROWS_HALF:(h + 1) * ROWS_HALF, :],
                                             cen_ps[p][h].rearrange("q (r c) -> q r c", c=W), ACT.Sign,
                                             saturate=False).then_inc(s_sign0, 1)
                else:
                    act.wait_ge(s_cen, 2 * p + 2)
                    for rows, cols, centred in centred_parts(p):
                        sign = nc.scalar.activation(grid[:, rows, :], centred.rearrange("q (r c) -> q r c", c=W),
                                                    ACT.Sign, saturate=False)
                    sign.then_inc(s_sign, 1)
                for rows, cols, centred in centred_parts(p):
                    keep = nc.scalar.activation(us[:, p, cols], centred, ACT.Copy)
                keep.then_inc(s_keep, 1)

            def keep_conv(p, halves=(0, 1)):
                for h in halves:
                    act.wait_ge(s_conv, 2 * p + h + 1)
                    nc.scalar.activation(conv16[:, p, h * HALF:(h + 1) * HALF], conv_ps[p][:, h, :],
                                         ACT.Copy).then_inc(s_c16, 1)

            def square(n, h=None):
                if n < PAIRS:
                    act.wait_ge(s_xc, 2 * n + 2 - (h == 0))
                else:
                    act.wait_ge(s_z, n - PAIRS + (h or 0) + 1)
                if n >= SQ_SLOTS and not h:
                    act.wait_ge(s_var, GROUP_OF[n - SQ_SLOTS] + 1)
                at = slice(0, TOK) if h is None else slice(h * HALF, (h + 1) * HALF)
                nc.scalar.activation(sq[:, n % SQ_SLOTS, at], us[:, n % PAIRS, at], ACT.Square).then_inc(s_sq, 1)

            def token_high(p):
                if p == ASIDE:
                    act.wait_ge(s_u_pool, 1)
                else:
                    act.wait_ge(s_u, tokens_ready(p))
                if p >= 2:
                    act.wait_ge(s_split[p - 2], 64)
                nc.scalar.activation(uh[:, p % 2, :], us[:, p, :], ACT.Copy).then_inc(s_uh, 1)

            def keep_deviation():
                act.wait_ge(s_sp, ASIDE + 1)
                act.wait_ge(s_prod, PAIRS - 1)
                nc.scalar.activation(dev, spread_ps[ASIDE].rearrange("q h n -> q (h n)"), ACT.Copy)\
                    .then_inc(s_dev, 1)

            for p in range(4):
                signs_of(p)
            keep_conv(0)
            signs_of(4)
            square(0)
            keep_conv(1)
            act.wait_ge(s_w1, 32)
            nc.scalar.activation(w1s[:, :, 0, :], w1f[:], ACT.Copy, scale=W1_SCALE).then_inc(s_w1h, 1)
            signs_of(5)
            keep_conv(2, (0,))
            square(1)
            keep_conv(2, (1,))
            signs_of(6)
            square(2)
            keep_conv(3)
            signs_of(7)
            for p in (4, 5):
                square(p - 1)
                keep_conv(p)
                token_high(p - 4)
            square(5)
            keep_conv(6, (0,))
            keep_deviation()
            keep_conv(6, (1,))
            keep_conv(7)
            square(6)
            for h in range(2):
                square(7, h)
            token_high(2)
            act.wait_ge(s_u_pool, 1)
            nc.scalar.activation(dev, us[:, ASIDE, :], ACT.Copy, accum_out=usum[:, ASIDE:ASIDE + 1]).then_inc(s_usum, 1)
            token_high(3)

            for n, (source, result, shift) in enumerate(((logit[:, 0, :], expo[:, 0, :], neg_top[:, 0:1]),
                                                         (logit[:, 1, :], expo[:, 1, :], neg_top[:, 1:2]),
                                                         (top_shifted[:], top_exp[:], 0.0))):
                act.wait_ge(s_route[f"shift{n + 1}"], 1)
                nc.scalar.activation(result, source, ACT.Exp, bias=shift,
                                     accum_out=total[:, n:n + 1]).then_inc(s_route_act, 1)

            nc.scalar.activation(warm[:], c32[:, C_ONES:C_ONES + 1], ACT.Gelu)

            def gelu(p, k, b):
                u = 2 * (2 * p + k) + b
                act.wait_ge(s_up, u + 1)
                if u == 0:
                    act.wait_ge(s_route["biases"], 1)
                if p >= 1:
                    act.wait_ge(s_down, 4 * (p - 1) + 2 * k + 2)
                col = k * 16 + b * PAIRS + p
                nc.scalar.activation(hid[:, k, b, :], hid_ps[b].rearrange("q h n -> q (h n)"), ACT.Gelu,
                                     bias=b1sel[:, col:col + 1], scale=1 / W1_SCALE).then_inc(s_gelu, 1)

            for p in range(PAIRS):
                gelu(p, 0, 0)
                gelu(p, 0, 1)
                gelu(p, 1, 0)
                if p >= 1:
                    square(PAIRS + p - 1)
                gelu(p, 1, 1)
                if 1 <= p <= PAIRS - EARLY:
                    token_high(p + EARLY - 1)
                elif p > PAIRS - EARLY:
                    act.wait_ge(s_res, p + 1)
                    nc.scalar.activation(xs[:, p, :], xs[:, p, :], ACT.Identity, bias=bet[:]).then_inc(s_beta, 1)
            for h in range(2):
                square(2 * PAIRS - 1, h)
            act.wait_ge(s_sp2, 2 * (PAIRS - 2) + 2)
            nc.scalar.activation(dev[:, 0:HALF], out_spread_ps(PAIRS - 2, 1), ACT.Identity, scale=gam[:])\
                .then_inc(s_gr, 1)

        @block.gpsimd
        def _(pool):
            words = signs[:].rearrange("q p n -> q (p n)").bitcast(F32)
            zw = REGIONS // 4
            nc.gpsimd.memset(words[:, 0:zw], 0.0).then_inc(s_zero, 1)
            nc.gpsimd.memset(words[:, zw:4 * zw], 0.0).then_inc(s_zero, 1)
            nc.gpsimd.memset(words[:, 4 * zw:], 0.0).then_inc(s_zero, 1)

            def product(p):
                if p > DVE_EDGES:
                    pool.wait_ge(s_sign, p)
                    pool.wait_ge(s_prod, p - 2)
                    edge_product(nc.gpsimd, p).then_inc(s_edge, 1)
                pool.wait_ge(s_edge, p + 2)
                sign_product(nc.gpsimd, p).then_inc(s_prod, 1)

            def token_low(p):
                pool.wait_ge(s_uh, p + 1)
                nc.gpsimd.tensor_tensor(out=ul[:, p % 2, :], in0=us[:, p, :], in1=uh[:, p % 2, :],
                                        op=ALU.subtract).then_inc(s_ul, 1)

            pool.wait_ge(s_zero, 3)
            for p in range(1, PAIRS):
                product(p)
            for p in range(EARLY):
                if p == 2:
                    pool.wait_ge(s_dev, 1)
                    nc.gpsimd.tensor_tensor(out=us[:, ASIDE, :], in0=us[:, ASIDE, :], in1=dev,
                                            op=ALU.mult).then_inc(s_u_pool, 1)
                token_low(p)

            table = w2f[:].rearrange("q e d -> q (e d)")

            def select_w2(p):
                for k in range(2):
                    for b in range(2):
                        col = k * 16 + b * PAIRS + p
                        e = pool.value_load(offs[0:1, 1, col:col + 1], min_val=0, max_val=(EXPERTS - 1) * CH)
                        nc.gpsimd.tensor_tensor(out=w2sel[:, k, b, p, :], in0=table[:, bass.ds(e, CH)],
                                                in1=picks[:, k, b * PAIRS + p:b * PAIRS + p + 1]
                                                .broadcast_to([128, CH]),
                                                op=ALU.mult).then_inc(s_w2s, 1)

            pool.wait_ge(s_route["offsets"], 2)
            pool.wait_ge(s_route["picks"], 1)
            pool.wait_ge(s_w2c, 4)
            select_w2(0)
            for p in range(PAIRS):
                if p + 1 < PAIRS:
                    select_w2(p + 1)
                nc.gpsimd.tensor_tensor(out=xs[:, p, :], in0=xs[:, p, :], in1=conv16[:, p, :],
                                        op=ALU.add).then_inc(s_res, 1)
                if 1 <= p <= PAIRS - EARLY:
                    token_low(p + EARLY - 1)

            def output(p, at=slice(0, TOK)):
                pool.wait_ge(s_beta, p - (PAIRS - 3) + 1)
                nc.gpsimd.tensor_tensor(out=xs[:, p, at], in0=us[:, p, at], in1=xs[:, p, at],
                                        op=ALU.add).then_inc(s_o_pool, 1)

            pool.wait_ge(s_zr, 2 * (PAIRS - 2))
            output(PAIRS - 3)
            second = us[:, PAIRS - 2, HALF:TOK]
            pool.wait_ge(s_gr, 1)
            nc.gpsimd.tensor_tensor(out=second, in0=second, in1=dev[:, 0:HALF], op=ALU.mult).then_inc(s_zr_pool, 1)
            pool.wait_ge(s_zr_pool, 1)
            output(PAIRS - 2, slice(HALF, TOK))
            pool.wait_ge(s_zr, 2 * (PAIRS - 2) + 1)
            output(PAIRS - 2, slice(0, HALF))
            pool.wait_ge(s_zr, 2 * (PAIRS - 2) + 2)
            output(PAIRS - 1, slice(0, HALF))

        @block.vector
        def _(dve):
            nc.vector.memset(zeros[:], 0.0).then_inc(s_zero_v, 1)
            nc.vector.memset(rstd_s[:], 0.0).then_inc(s_zero_v, 1)
            nc.vector.memset(ublk[:], 0.0).then_inc(s_ublk, 1)

            def edges(p):
                dve.wait_ge(s_sign, p)
                if p == 2:
                    dve.wait_ge(s_prod0, 2)
                elif p > 2:
                    dve.wait_ge(s_prod, p - 2)
                edge_product(nc.vector, p).then_inc(s_edge, 1)

            def order_conv_weights():
                V = nc.vector
                dve.wait_ge(s_cw_sign, 1)
                V.tensor_tensor(out=cwp[:], in0=cws[:, :, 0, :], in1=cws[:, :, 1, :],
                                op=ALU.mult).then_inc(s_cw_prep, 1)
                dve.wait_ge(s_cw_prep, 1)
                for b in range(2):
                    V.scalar_tensor_tensor(out=cwo[:, b, :, 1, b, :], in0=cwp[:], scalar=-0.5, in1=cws[:, :, 2, :],
                                           op0=ALU.mult, op1=ALU.mult).then_inc(s_cw_ord, 1)
                V.tensor_scalar(cwo[:, 0, :, 0, :, :], cws[:, :, 0:2, :], 0.5, None,
                                ALU.mult).then_inc(s_cw_ord, 1)
                for t in range(2):
                    V.tensor_scalar(cwo[:, 1, :, 0, t, :], cws[:, :, 1 - t, :], 0.5, None,
                                    ALU.mult).then_inc(s_cw_ord, 1)
                for b in range(2):
                    V.tensor_scalar(cwo[:, b, :, 1, 1 - b, :], cws[:, :, 2, :], 0.5, None,
                                    ALU.mult).then_inc(s_cw_ord, 1)

            def expert_weights():
                dve.wait_ge(s_w1h, 1)
                nc.vector.scalar_tensor_tensor(out=w1s[:, :, 1, :], in0=w1f[:], scalar=W1_SCALE, in1=w1s[:, :, 0, :],
                                               op0=ALU.mult, op1=ALU.subtract).then_inc(s_w1l, 1)
                dve.wait_ge(s_w2, 32)
                nc.vector.tensor_reduce(w2m[:], w2f[:], AX.X, ALU.add).then_inc(s_w2c, 1)
                nc.vector.tensor_reduce(b2m[:], b2f[:], AX.X, ALU.add).then_inc(s_w2c, 1)
                dve.wait_ge(s_w2c, 2)
                mean = w2m[:].rearrange("q (e o) -> q e o", o=1).broadcast_to([128, EXPERTS, CH])
                nc.vector.scalar_tensor_tensor(out=w2f[:], in0=mean, scalar=-1.0 / CH, in1=w2f[:],
                                               op0=ALU.mult, op1=ALU.add).then_inc(s_w2c, 1)
                nc.vector.scalar_tensor_tensor(out=b2f[:], in0=b2m[:].broadcast_to([EXPERTS, CH]), scalar=-1.0 / CH,
                                               in1=b2f[:], op0=ALU.mult, op1=ALU.add).then_inc(s_w2c, 1)

            steps = [0]

            def step(i):
                steps[0] += 1
                i.then_inc(s_newton, 1)
                dve.wait_ge(s_newton, steps[0])

            def views(g):
                return (stat[:, i, 0:8 * len(GROUP[g]), :] for i in range(4))

            def estimate(g):
                V, run = nc.vector, len(GROUP[g]) * QUARTER
                v, y, a, b = views(g)
                dve.wait_ge(s_var, g + 1)
                V.transpose(var_t[:, 0:run], var_ps[:, 0:run]).then_inc(s_vt, 1)
                dve.wait_ge(s_vt, g + 1)
                step(V.tensor_scalar(v, var_t[:, 0:run].rearrange("q (a c) -> q a c", c=32)[:, :, 0:2],
                                     RSTD_SCALE ** -2, EPS_LN * RSTD_SCALE ** -2, ALU.mult, ALU.add))
                step(V.tensor_scalar(y.bitcast(I32), v.bitcast(I32), -0.5, MAGIC, ALU.mult, ALU.add))
                step(V.tensor_tensor(out=a, in0=y, in1=y, op=ALU.mult))
                step(V.tensor_tensor(out=a, in0=a, in1=v, op=ALU.mult))
                step(V.tensor_scalar(b, a, 0.375, -1.25, ALU.mult, ALU.add))
                step(V.tensor_tensor(out=b, in0=b, in1=a, op=ALU.mult))
                step(V.scalar_tensor_tensor(out=y, in0=b, scalar=1.875, in1=y, op0=ALU.add, op1=ALU.mult))

            def refine(g):
                V, n = nc.vector, 8 * len(GROUP[g])
                v, y, a, b = views(g)
                step(V.tensor_tensor(out=a, in0=y, in1=y, op=ALU.mult))
                step(V.scalar_tensor_tensor(out=a, in0=a, scalar=-0.5, in1=v, op0=ALU.mult, op1=ALU.mult))
                if g == 0:
                    dve.wait_ge(s_zero_v, 2)
                V.scalar_tensor_tensor(out=rstd_s[:, 0:n, 0:2], in0=a, scalar=1.5, in1=y, op0=ALU.add,
                                       op1=ALU.mult).then_inc(s_high, 1)
                step(V.scalar_tensor_tensor(out=b, in0=a, scalar=1.5, in1=y, op0=ALU.add, op1=ALU.mult))
                dve.wait_ge(s_high, g + 1)
                step(V.tensor_tensor(out=rstd_s[:, 0:n, 2:4], in0=b, in1=rstd_s[:, 0:n, 0:2], op=ALU.subtract))
                if 2 <= g <= GROUPS + 1:
                    dve.wait_ge(s_sp, GROUP[g - 2][-1] + 1)
                elif g > GROUPS + 1:
                    dve.wait_ge(s_sp2, 2 * (g - 1 - GROUPS))
                V.transpose(rstd_t[:, g % 2, 0:32 * n],
                            rstd_s[:, 0:n, :].rearrange("q a c -> q (a c)")).then_inc(s_rt, 1)

            def inverse_deviations(g):
                estimate(g)
                refine(g)

            def residual(p):
                for h in range(2):
                    half = us[:, p, h * HALF:(h + 1) * HALF]
                    dve.wait_ge(s_cc, 2 * p + h + 1)
                    nc.vector.tensor_tensor(out=half, in0=half, in1=conv_ps[p][:, h, :], op=ALU.add).then_inc(s_xc, 1)

            def tokens(p):
                dve.wait_ge(s_sp, p + 1)
                nc.vector.scalar_tensor_tensor(out=us[:, p, :], in0=us[:, p, :], scalar=1.0,
                                               in1=spread_ps[p].rearrange("q h n -> q (h n)"),
                                               op0=ALU.mult, op1=ALU.mult, accum_out=usum[:, p:p + 1]).then_inc(s_u, 1)

            order_conv_weights()
            for h in range(2):
                dve.wait_ge(s_sign0, h + 1)
                edge_product(nc.vector, 0, h).then_inc(s_edge, 1)
                dve.wait_ge(s_edge, h + 1)
                sign_product(nc.vector, 0, h).then_inc(s_prod0, 1)
            dve.wait_ge(s_cw_tr, 1)
            nc.vector.tensor_copy(cwT[:].rearrange("q b r t o -> q (b r t o)"),
                                  early_ps[:, 0:384].bitcast(F16)).then_inc(s_cw_done, 1)
            for p in range(1, DVE_EDGES + 1):
                edges(p)
            for p in range(4):
                residual(p)
                if p == 1:
                    expert_weights()
                elif p == 2:
                    inverse_deviations(0)
            tokens(0)
            tokens(1)
            residual(4)
            estimate(1)
            residual(5)
            refine(1)
            estimate(2)
            tokens(2)
            residual(6)
            refine(2)
            residual(7)
            tokens(4)
            inverse_deviations(3)
            for p in range(5, PAIRS):
                tokens(p)

            dve.wait_ge(s_u, PAIRS - 1)
            dve.wait_ge(s_usum, 1)
            dve.wait_ge(s_ublk, 1)
            nc.vector.tensor_copy(ublk[LO, 0, :], usum[LO, :]).then_inc(s_ublk, 1)
            nc.vector.tensor_copy(ublk[HI, 1, :], usum[HI, :]).then_inc(s_ublk, 1)
            V = nc.vector

            def then(name, i, value=1):
                i.then_inc(s_route[name], 1)
                dve.wait_ge(s_route[name], value)

            dve.wait_ge(s_route_pe, 1)
            then("logits", V.scalar_tensor_tensor(out=logit[:, 0, :], in0=early_ps[0:16, 0:8], scalar=1.0 / TOK,
                                                  in1=brs[:], op0=ALU.mult, op1=ALU.add))
            V.tensor_reduce(neg_top[:, 0:1], logit[:, 0, :], AX.X, ALU.max, negate=True).then_inc(s_route["shift1"], 1)
            dve.wait_ge(s_route_act, 1)
            then("inverse", V.reciprocal(inverse[:, 0:1], total[:, 0:1]), 1)
            V.tensor_scalar(weight[:, 0, :], expo[:, 0, :], inverse[:, 0:1], None,
                            ALU.mult).then_inc(s_route["weights1"], 1)
            dve.wait_ge(s_route_pe, 2)
            then("relief", V.reciprocal(relief[:], early_ps[0:16, 8:16]))
            then("scaled", V.scalar_tensor_tensor(out=logit[:, 1, :], in0=relief[:], scalar=1.0, in1=weight[:, 0, :],
                                                  op0=ALU.min, op1=ALU.mult))
            V.tensor_reduce(neg_top[:, 1:2], logit[:, 1, :], AX.X, ALU.max, negate=True).then_inc(s_route["shift2"], 1)
            dve.wait_ge(s_route_act, 2)
            V.max(top8[:], expo[:, 1, :]).then_inc(s_route["top"], 1)
            V.reciprocal(inverse[:, 1:2], total[:, 1:2]).then_inc(s_route["inverse"], 1)
            dve.wait_ge(s_route["top"], 1)
            V.max_index(top8_at[:], top8[:], expo[:, 1, :]).then_inc(s_route["top"], 1)
            dve.wait_ge(s_route["inverse"], 2)
            V.tensor_scalar(top_shifted[:], top8[:, 0:2], top8[:, 0:1], inverse[:, 1:2], ALU.subtract,
                            ALU.mult).then_inc(s_route["shift3"], 1)
            dve.wait_ge(s_route["top"], 2)
            eye = c32[0:16, C_EYE:C_EYE + 16].rearrange("q (o n) -> q o n", o=1).broadcast_to([16, 2, 16])
            V.tensor_tensor(out=diag[:, 1, :, :], in0=eye,
                            in1=top8_at[:, 0:2].rearrange("q (k o) -> q k o", o=1).broadcast_to([16, 2, 16]),
                            op=ALU.mult).then_inc(s_route["diagonals"], 1)
            dve.wait_ge(s_route_pe, 3)
            V.tensor_scalar(offs[0:1, 0, :], picks_ps[1][0:1, :], float(2 * FFN), None,
                            ALU.mult).then_inc(s_route["offsets"], 1)
            V.tensor_scalar(hot[:], picks_ps[1][0:8, :], c32[0:8, C_PART:C_PART + 1], None,
                            ALU.is_equal).then_inc(s_route["hot"], 1)
            V.tensor_scalar(offs[0:1, 1, :], picks_ps[1][0:1, :], float(CH), None,
                            ALU.mult).then_inc(s_route["offsets"], 1)
            dve.wait_ge(s_route_act, 3)
            then("inverse", V.reciprocal(inverse[:, 2:3], total[:, 2:3]), 3)
            V.scalar_tensor_tensor(out=diag[:, 0, :, :], in0=eye, scalar=inverse[:, 2:3],
                                   in1=top_exp[:].rearrange("q (k o) -> q k o", o=1).broadcast_to([16, 2, 16]),
                                   op0=ALU.mult, op1=ALU.mult).then_inc(s_route["diagonals"], 1)
            dve.wait_ge(s_route_pe, 4)
            V.tensor_copy(b1sel[:], b1_ps).then_inc(s_route["biases"], 1)
            dve.wait_ge(s_route_pe, 5)
            then("picks", V.tensor_copy(picks[:].rearrange("q k n -> q (k n)"), picks_ps[0]))
            dve.wait_ge(s_route["hot"], 1)
            then("dense", V.tensor_tensor(out=wden[:].rearrange("q k n -> q (k n)"), in0=hot[:],
                                          in1=picks[0:8, :, :].rearrange("q k n -> q (k n)"), op=ALU.mult))
            then("dense", V.tensor_tensor(out=wden[:, 0, :], in0=wden[:, 0, :], in1=wden[:, 1, :], op=ALU.add), 2)
            dve.wait_ge(s_route_pe, 6)
            then("biases", V.tensor_copy(b2sel[:], b2_ps), 2)

            last = PAIRS - 1

            def mixture(p, h=None):
                at = slice(0, TOK) if h is None else slice(h * HALF, (h + 1) * HALF)
                dve.wait_ge(s_down, 4 * p + 4 - (h == 0))
                nc.vector.scalar_tensor_tensor(out=us[:, p, at], in0=y_ps.rearrange("q h n -> q (h n)")[:, at],
                                               scalar=b2sel[:, p:p + 1], in1=us[:, p, at],
                                               op0=ALU.add, op1=ALU.add).then_inc(s_z, 1)

            def normalise(p, h):
                dve.wait_ge(s_sp2, 2 * p + h + 1)
                half = us[:, p, h * HALF:(h + 1) * HALF]
                spread = out_spread_ps(p, h)
                nc.vector.scalar_tensor_tensor(out=half, in0=half, scalar=gam[:], in1=spread,
                                               op0=ALU.mult, op1=ALU.mult).then_inc(s_zr, 1)

            def output(p, h=None):
                at = slice(0, TOK) if h is None else slice(h * HALF, (h + 1) * HALF)
                dve.wait_ge(s_zr, 2 * p + 2 - (p == last))
                dve.wait_ge(s_res, p + 1)
                if p < PAIRS - 3:
                    nc.vector.scalar_tensor_tensor(out=xs[:, p, at], in0=us[:, p, at], scalar=bet[:],
                                                   in1=xs[:, p, at], op0=ALU.add, op1=ALU.add).then_inc(s_o, 1)
                else:
                    dve.wait_ge(s_beta, p - (PAIRS - 3) + 1)
                    nc.vector.tensor_tensor(out=xs[:, p, at], in0=us[:, p, at], in1=xs[:, p, at],
                                            op=ALU.add).then_inc(s_o, 1)

            for p in range(PAIRS):
                if p >= 1:
                    mixture(p - 1)
                if p >= 2:
                    normalise(p - 2, 0)
                    normalise(p - 2, 1)
                    if p < last:
                        output(p - 2)
                if 1 <= p < last:
                    inverse_deviations(GROUPS + p - 1)
            estimate(GROUPS + last - 1)
            for h in range(2):
                mixture(last, h)
            refine(GROUPS + last - 1)
            estimate(GROUPS + last)
            refine(GROUPS + last)
            normalise(last - 1, 0)
            for h in range(2):
                normalise(last, h)
            output(last, 1)


_INS = ["x", "L0_conv_weight", "L0_ffn_Wr", "L0_ffn_br", "L0_ffn_W1", "L0_ffn_b1", "L0_ffn_W2", "L0_ffn_b2",
        "L0_ffn_gamma", "L0_ffn_beta"]


def kernel(**inputs):
    import concourse.bacc as _bacc
    from concourse import mybir as _mybir
    from concourse.bass_utils import run_bass_kernel_spmd as _run

    nc = _bacc.Bacc("TRN2", target_bir_lowering=False, num_devices=1)
    arrays, args = {}, []
    c32, c16 = constants()
    for name, a in [(n, np.ascontiguousarray(inputs[n])) for n in _INS] + [("const32", c32), ("const16", c16)]:
        arrays[f"in_{name}"] = a
        args.append(nc.dram_tensor(f"in_{name}", a.shape, _mybir.dt.from_np(a.dtype), kind="ExternalInput").ap())
    args.append(nc.dram_tensor("out_0", (N_IMG, CH, H, W), _mybir.dt.float32, kind="ExternalOutput").ap())
    metaformer(nc, *args)
    return _run(nc, [arrays], core_ids=[0]).results[0]["out_0"]
```
